# Optimizing a Trainium2 kernel written in Bass

```python
import numpy as np
import jax
import jax.numpy as jnp

def _softmax(x, axis=-1):
    return jax.nn.softmax(x, axis=axis)

def _gelu(x):
    return jax.nn.gelu(x, approximate=True)

def _silu(x):
    return jax.nn.silu(x)

def _sigmoid(x):
    return jax.nn.sigmoid(x)

def _layernorm(x, axis=-1, eps=1e-05):
    m = jnp.mean(x, axis=axis, keepdims=True)
    v = jnp.var(x, axis=axis, keepdims=True)
    return (x - m) / jnp.sqrt(v + eps)

def _scatter_add(tgt, idx, src, axis=0):
    return tgt.at[idx].add(src)

def _segment_sum(src, seg, n):
    return jax.ops.segment_sum(src, seg, n)
kernel_name = 'mk_adj_preln_d1_adj_r2_b011e8'

def setup_inputs(seed: int=0):
    np.random.seed(seed)
    _w = jnp.asarray

    def _rec_inputs():
        import jax
        import jax.numpy as jnp
        _gk = jax.random.key(seed)
        x = -0.0005207 + 1.001 * jax.random.normal(jax.random.fold_in(_gk, 1), (8192, 128), jnp.float32)
        _a = jax.random.bernoulli(jax.random.fold_in(_gk, 2), 0.00195312, (8192, 8192))
        _af = _a.astype(jnp.float32)
        adj = _af
        return (x, adj)
    x, adj = _rec_inputs()

    def _L0_gnn_setup():
        import jax, jax.numpy as jnp
        import numpy as np
        N = 8192
        U = 128
        AVG_DEGREE = 32
        key = jax.random.key(seed)
        kx, ka, kw = jax.random.split(key, 3)
        x = jax.random.normal(kx, (N, U), dtype=jnp.float32)
        adj = (jax.random.uniform(ka, (N, N)) < AVG_DEGREE / N).astype(jnp.float32)
        W = jax.random.normal(kw, (U, U), dtype=jnp.float32) * 0.05
        b = jnp.zeros((U,), dtype=jnp.float32)
        return {'x': x, 'adj': adj, 'W': W, 'b': b}
    _L0_gnn_all = _L0_gnn_setup()
    _L0_gnn_in = {k: v for k, v in _L0_gnn_all.items() if k in ('W', 'b')}
    del _L0_gnn_all
    return {'x': x, 'adj': adj, 'L0_gnn_W': _L0_gnn_in['W'], 'L0_gnn_b': _L0_gnn_in['b']}

def reference(x, adj, L0_gnn_W, L0_gnn_b):
    import jax
    import jax.numpy as jnp

    def _L0_gnn_ref(x, adj, W, b):
        import jax, jax.numpy as jnp
        import numpy as np
        N = 8192
        U = 128
        AVG_DEGREE = 32
        adj = jax.lax.stop_gradient(adj)
        neigh1 = adj @ x
        x1 = jax.nn.swish(neigh1 @ W + b)
        neigh2 = adj @ x1
        x2 = jax.nn.swish(neigh2 @ W + b)
        return x2
    h = jnp.maximum(_layernorm(x, axis=-1), 0.0)
    x = x + _L0_gnn_ref(h, adj, L0_gnn_W, L0_gnn_b)
    return x

_drawn_inputs = setup_inputs


def setup_inputs(seed=0):
    import zlib

    import numpy as np

    out = dict(_drawn_inputs(seed))
    spreads = {'L0_gnn_b': (0.0, 0.1)}
    factors = {}
    for name, (base, spread) in spreads.items():
        noise = np.random.default_rng([zlib.crc32(name.encode()), seed]).standard_normal(out[name].shape)
        drawn = base * np.exp(spread * noise) if base else spread * noise
        out[name] = jnp.asarray(drawn.astype(out[name].dtype))
    for name, factor in factors.items():
        out[name] = (out[name] * factor).astype(out[name].dtype)
    return out
```

```python
from contextlib import ExitStack

import concourse.bass as bass
from concourse import mybir

P = 128
N = 8192
U = 128
KT = N // P
NB = 512
RB = N // NB
TPB = NB // P
TPC = 4
CHUNK = TPC * NB
CH = KT // TPC
GT = 8
GR = KT // GT
SLOTS = 4
F8_SLOTS = 4
NS = 4
RPS = RB // NS
WORDS = NB // 4
ONE8 = 2.0
PART_SCALE = 256.0
UNSCALE = 1.0 / (ONE8 * PART_SCALE)
LIMIT = 32768.0
EPS = 1e-5
START = 1
LN_PIECES = 4
LN_T = KT // LN_PIECES

HALVES_AFTER = {0: [], 1: [2, 5], 2: [0, 1, 3, 4, 5, 6], 3: [0, 1, 2, 3, 3, 4, 5, 6, 6, 7]}


def sums_of(stage):
    if stage == 0:
        return []
    return [[(k, stage - 1) for k in range(stage)]] + [[(stage - 1, n)] for n in range(stage - 1)]


def units_of(stage):
    return [unit for one in sums_of(stage) for unit in one]


UNIT_BASE = [RPS * sum(len(units_of(s)) for s in range(stage)) for stage in range(NS + 1)]
COPY_BASE = [RPS * max(stage - 1, 0) for stage in range(NS + 1)]
ADD_BASE = [RPS * sum(max(s - 1, 0) for s in range(stage)) for stage in range(NS + 1)]


def packed_slot(k, n):
    if n < NS - 1:
        return n * NS + k
    return [packed_slot(0, 0), packed_slot(1, 0), packed_slot(0, 1), packed_slot(1, 1)][k]


def graph_block(nc, x, adj, w, b, out):
    f32, f16, f8 = mybir.dt.float32, mybir.dt.float16, mybir.dt.float8e4
    u32 = mybir.dt.uint32
    ALU = mybir.AluOpType
    ACT = mybir.ActivationFunctionType
    AX = mybir.AxisListType

    x_v = x.rearrange("(p t) u -> p t u", t=KT)
    out_v = out.rearrange("(p t) u -> p t u", t=KT)

    ctx = ExitStack()
    with ctx:
        def sb(name, shape, dt):
            return ctx.enter_context(nc.sbuf_tensor(name, shape, dt))

        def pb(name):
            return ctx.enter_context(nc.psum_tensor(name, [P, NB], f32))

        def sem(name):
            return ctx.enter_context(nc.semaphore(name))

        ring = sb("adj_ring", [P, SLOTS, CHUNK], f32)
        x_all = ring[:, :, :].rearrange("p s (t u) -> p (s t) u", u=U)
        f8ring = sb("f8_ring", [P, F8_SLOTS, GT * NB], f8)
        packed = sb("packed", [P, 12, 2, RPS, WORDS], u32)
        x_stage = packed[:, 4:12].rearrange("p a b c w -> p (a b c w)").bitcast(f32)\
            .rearrange("p (t u) -> p t u", u=U)
        h_parts = sb("h_parts", [P, 2, KT, U], f16)
        h_hi, h_lo = h_parts[:, 0], h_parts[:, 1]
        x1_parts = sb("x1_parts", [P, 2, KT, U], f16)
        x1_hi, x1_lo = x1_parts[:, 0], x1_parts[:, 1]
        acc = sb("acc", [P, RB - RPS, NB], f32)
        unpacked = sb("unpacked", [P, 2, GT, 2, WORDS], u32)
        folded = sb("folded", [P, 4 * WORDS], u32)
        w_sb = sb("w_sb", [P, U], f32)
        b_sb = sb("b_sb", [P, U], f32)
        neigh = sb("neigh", [P, NB], f32)
        act = neigh
        stats = sb("stats", [P, LN_T, 6], f32)
        ln_a = sb("ln_a", [P, LN_T], f32)
        ln_b = sb("ln_b", [P, LN_T], f32)
        ln_c = sb("ln_c", [P, LN_T], f32)
        ln_r = sb("ln_r", [P, LN_T], f32)
        ln_n = sb("ln_n", [P, LN_T], f32)
        strays = sb("strays", [P, RB * CH], f32)
        tops = sb("tops", [P, RB], f32)
        found = sb("found", [P, 4], f32)
        ones = sb("ones", [P, 1], f32)
        flag = sb("flag", [1, 1], u32)
        neigh_t = [f8ring[:, i].bitcast(f32)[:, 0:NB] for i in range(2)]
        act_t = [f8ring[:, 2 + i].bitcast(f32)[:, 0:NB] for i in range(2)]

        g_h = h_parts[:, :, :, :].rearrange("p a t u -> p (a t u)").bitcast(f32)\
            .rearrange("p (t u) -> p t u", u=U)
        g_x1 = x1_parts[:, :, :, :].rearrange("p a t u -> p (a t u)").bitcast(f32)\
            .rearrange("p (t u) -> p t u", u=U)
        g_act = act_t[0]

        bank_first = pb("bank_first")
        bank_z = pb("bank_z")
        bank_sum = [pb(f"bank_sum{i}") for i in range(3)]
        bank_flag = pb("bank_flag")

        x_loaded = [sem(f"x_loaded{i}") for i in range(LN_PIECES)]
        w_loaded = sem("w_loaded")
        chunk_loaded = [sem(f"chunk_loaded{i}") for i in range(SLOTS)]
        f8_made = sem("f8_made")
        chunk_checked = sem("chunk_checked")
        pack_steps = sem("pack_steps")
        ln_steps = sem("ln_steps")
        ln_vars = sem("ln_vars")
        ln_roots = sem("ln_roots")
        ln_scales = sem("ln_scales")
        h_full = sem("h_full")
        h_high = sem("h_high")
        h_ready = sem("h_ready")
        groups_done = sem("groups_done")
        neigh_copied = sem("neigh_copied")
        z_summed = sem("z_summed")
        z_biased = sem("z_biased")
        act_done = sem("act_done")
        x1_high = sem("x1_high")
        x1_ready = sem("x1_ready")
        unit_unpacked = sem("unit_unpacked")
        unit_used = sem("unit_used")
        acc_copied = sem("acc_copied")
        acc_added = sem("acc_added")
        residual_added = sem("residual_added")
        x_reloaded = sem("x_reloaded")
        out_stored = sem("out_stored")
        scalar_passed = sem("scalar_passed")
        tensor_passed = sem("tensor_passed")
        flag_steps = sem("flag_steps")
        flag_summed = sem("flag_summed")
        flag_ready = sem("flag_ready")

        g_x_loaded = [sem(f"g_x_loaded{i}") for i in range(LN_PIECES)]
        g_ln_steps = sem("g_ln_steps")
        g_ln_vars = sem("g_ln_vars")
        g_ln_roots = sem("g_ln_roots")
        g_ln_scales = sem("g_ln_scales")
        g_h_full = sem("g_h_full")
        g_chunk_loaded = [sem(f"g_chunk_loaded{i}") for i in range(SLOTS)]
        g_chunk_used = sem("g_chunk_used")
        g_copied = sem("g_copied")
        g_biased = sem("g_biased")
        g_swished = sem("g_swished")
        g_z_summed = sem("g_z_summed")
        g_x_reloaded = sem("g_x_reloaded")
        g_added = sem("g_added")
        g_stored = sem("g_stored")

        def f8_tile(group_slot, t):
            return f8ring[:, group_slot, t * NB:(t + 1) * NB]

        def unit_tile(slot, half, t):
            return unpacked[:, slot, t, half, :].bitcast(f8)

        def tiles(buf, rb):
            return buf[:, bass.ds(rb * TPB, TPB), :]

        def as_tiles(buf):
            return buf.rearrange("p (t u) -> p t u", u=U)

        def stand_alone(eng, passed):
            eng.sem_inc(passed, 1)

        def unit_slot(unit_in_stage, stage):
            return unit_in_stage % 2 if stage < NS else (unit_in_stage + 1) % 2

        def halves_at(stage, group):
            found_halves = []
            where = [(s, i, len(one)) for s, one in enumerate(sums_of(stage)) for i in range(len(one))]
            for q, g in enumerate(HALVES_AFTER[stage]):
                if g == group:
                    s, i, n = where[q // 2]
                    found_halves.append((q // 2, q % 2, i == 0 and q % 2 == 0, i == n - 1 and q % 2 == 1, s))
            return found_halves

        def stages(eng, body):
            body(0, 0)
            with eng.Fori(1, RPS) as r:
                body(0, r)
            for stage in range(1, NS):
                with eng.Fori(0, RPS) as r:
                    body(stage, r)

        block = ctx.enter_context(nc.Block())

        @block.sync
        def _(sp):
            for i in range(LN_PIECES):
                sp.dma_start(x_stage[:, i * LN_T:(i + 1) * LN_T, :],
                             x_v[:, i * LN_T:(i + 1) * LN_T, :]).then_inc(x_loaded[i], 16)
                if i == 0:
                    sp.dma_start(ring[:, 0, :], adj[0, 0]).then_inc(chunk_loaded[0], 16)
                    sp.dma_start(w_sb[:, :], w).then_inc(w_loaded, 16)
                    sp.dma_start(b_sb[:, :], b.partition_broadcast(P)).then_inc(w_loaded, 16)
                    sp.dma_start(ring[:, 1, :], adj[0, 1]).then_inc(chunk_loaded[1], 16)

            def loads(stage, r):
                first = stage == 0 and isinstance(r, int)
                rb = r + RPS * stage
                for c in range(CH):
                    if first and c < 2:
                        continue
                    if not (first and c < SLOTS):
                        sp.wait_ge(chunk_checked, rb * CH + (c - SLOTS + 1))
                    sp.dma_start(ring[:, c % SLOTS, :], adj[rb, c]).then_inc(chunk_loaded[c % SLOTS], 16)

            stages(sp, loads)
            sp.wait_ge(chunk_checked, RB * CH)
            sp.dma_start(x_all, x_v).then_inc(x_reloaded, 16)

            def stores(n, t):
                sp.wait_ge(residual_added, t + 1)
                sp.dma_start(tiles(out_v, n), tiles(x_all, n)).then_inc(out_stored, 16)

            with sp.Fori(0, RPS) as i:
                stores(i + (RB - RPS), i)
            with sp.Fori(0, RB - RPS) as i:
                stores(i, i + RPS)
            sp.wait_ge(out_stored, 16 * RB)

            sp.wait_ge(flag_ready, 1)
            general = sp.value_load(flag[0:1, 0:1], min_val=0, max_val=1)
            with sp.If(general == 1):
                for i in range(LN_PIECES):
                    s = slice(i * LN_T, (i + 1) * LN_T)
                    sp.dma_start(g_h[:, s, :], x_v[:, s, :]).then_inc(g_x_loaded[i], 16)
                for rnd in range(2):
                    with sp.Fori(0, RB) as rb:
                        for c in range(CH):
                            sp.wait_ge(g_chunk_used, rb * CH + (rnd * RB * CH + c + 1))
                            sp.dma_start(ring[:, c % SLOTS, :], adj[rb, c])\
                              .then_inc(g_chunk_loaded[c % SLOTS], 16)
                    if rnd == 0:
                        sp.wait_ge(g_chunk_used, RB * CH + SLOTS)
                        sp.dma_start(g_h, x_v).then_inc(g_x_reloaded, 16)

        @block.scalar
        def _(sc):
            def normalize(i, part, variances, roots, scales, full):
                sc.wait_ge(variances, i + 1)
                nc.scalar.activation(ln_c[:, :], ln_b[:, :], ACT.Sqrt).then_inc(roots, 1)
                sc.wait_ge(scales, i + 1)
                for t in range(LN_T):
                    last = nc.scalar.activation(part[:, t, :], part[:, t, :], ACT.Relu,
                                                bias=ln_n[:, t:t + 1], scale=ln_r[:, t:t + 1])
                last.then_inc(full, 1)

            def ln_piece(i):
                part = x_stage[:, i * LN_T:(i + 1) * LN_T, :]
                normalize(i, part, ln_vars, ln_roots, ln_scales, h_full)
                sc.wait_ge(h_full, i + 1)
                nc.scalar.activation(h_hi[:, i * LN_T:(i + 1) * LN_T, :], part, ACT.Copy)\
                  .then_inc(h_high, 1)

            def copy_neigh(done):
                sc.wait_ge(groups_done, done * GR)
                sc.wait_ge(x1_ready, done - 1 + START)
                nc.scalar.activation(neigh[:, :], bank_first[:, :], ACT.Copy, scale=UNSCALE)\
                  .then_inc(neigh_copied, 1)

            def swish(done):
                sc.wait_ge(z_biased, done + START)
                nc.scalar.activation(act[:, :], act[:, :], ACT.Silu).then_inc(act_done, 1)

            def row_block(stage, r):
                first = stage == 0 and isinstance(r, int)
                rb = r + RPS * stage
                for g in range(GR):
                    if first and g % 2 == 0:
                        ln_piece(g // 2)
                    for half in range(2):
                        c = 2 * g + half
                        if half == 0 and not (first and g < F8_SLOTS):
                            sc.wait_ge(groups_done, rb * GR + (g - F8_SLOTS + 1))
                            sc.wait_ge(pack_steps, rb * (3 * GR) + (3 * (g - F8_SLOTS) + 1))
                        sc.wait_ge(chunk_loaded[c % SLOTS], rb * (16 * CH // SLOTS) + 16 * (c // SLOTS + 1))
                        stand_alone(sc, scalar_passed)
                        nc.scalar.activation(f8ring[:, g % F8_SLOTS, half * CHUNK:(half + 1) * CHUNK],
                                             ring[:, c % SLOTS, :], ACT.Copy, scale=ONE8,
                                             saturate=False).then_inc(f8_made, 1)
                    if g == 0 and not first:
                        copy_neigh(rb)
                    if g == 2 and not first:
                        swish(rb)
                if stage:
                    sc.wait_ge(unit_used, r * len(units_of(stage)) + (UNIT_BASE[stage] + stage + START))
                    nc.scalar.activation(acc[:, bass.ds(r + RPS * (stage - 1), 1), :], bank_sum[0][:, :],
                                         ACT.Copy, scale=UNSCALE).then_inc(acc_copied, 1)

            sc.sem_inc(acc_copied, START)
            stages(sc, row_block)
            copy_neigh(RB)
            swish(RB)

            def tail_swish(e, t):
                sc.wait_ge(z_biased, t + (RB + 1 + START))
                nc.scalar.activation(act_t[e % 2], act_t[e % 2], ACT.Silu).then_inc(act_done, 1)

            with sc.Fori(0, RPS // 2) as i:
                for e in range(2):
                    t = i * 2 + e
                    if e == 1:
                        tail_swish(0, i * 2)
                    sc.wait_ge(unit_used, t * NS + (UNIT_BASE[NS] + NS + START))
                    sc.wait_ge(z_summed, t + (RB - 1))
                    nc.scalar.activation(neigh_t[e], bank_sum[e][:, :], ACT.Copy, scale=UNSCALE)\
                      .then_inc(acc_copied, 1)
                tail_swish(1, i * 2 + 1)
            with sc.Fori(0, (RB - RPS) // 4) as i:
                for e in range(4):
                    tail_swish(e, i * 4 + (e + RPS))

            sc.wait_ge(flag_ready, 1)
            general = sc.value_load(flag[0:1, 0:1], min_val=0, max_val=1)
            with sc.If(general == 1):
                sc.sem_inc(g_copied, START)
                sc.sem_inc(g_swished, START)
                for i in range(LN_PIECES):
                    normalize(i, g_h[:, i * LN_T:(i + 1) * LN_T, :], g_ln_vars, g_ln_roots, g_ln_scales,
                              g_h_full)
                for rnd in range(2):
                    with sc.Fori(0, RB) as rb:
                        done = rb + rnd * RB
                        sc.wait_ge(g_chunk_used, rb * CH + ((rnd * RB + 1) * CH + SLOTS))
                        nc.scalar.activation(neigh[:, :], bank_first[:, :], ACT.Copy).then_inc(g_copied, 1)
                        sc.wait_ge(g_biased, done + (1 + START))
                        to = as_tiles(g_act) if rnd else tiles(g_x1, rb)
                        nc.scalar.activation(to, as_tiles(g_act), ACT.Silu).then_inc(g_swished, 1)
                        if rnd:
                            sc.wait_ge(g_added, rb + 1)
                            sc.dma_start(tiles(out_v, rb), tiles(g_h, rb)).then_inc(g_stored, 16)
                sc.wait_ge(g_stored, 16 * RB)

        @block.vector
        def _(ve):
            def statistics(i, part, factor, loaded, counted, variances, roots, scales, full):
                steps = [i * 7]

                def link(instruction):
                    instruction.then_inc(counted, 1)
                    steps[0] += 1
                    ve.wait_ge(counted, steps[0])

                ve.wait_ge(loaded[i], 16)
                if i:
                    ve.wait_ge(full, i)
                for t in range(LN_T):
                    last = nc.vector.bn_stats(stats[:, t, :], part[:, t, :])
                link(last)
                nc.vector.tensor_tensor(ln_a[:, :], stats[:, :, 1], stats[:, :, 4], ALU.subtract)
                nc.vector.tensor_tensor(ln_n[:, :], stats[:, :, 1], stats[:, :, 4], ALU.add)
                link(nc.vector.tensor_tensor(ln_b[:, :], stats[:, :, 2], stats[:, :, 5], ALU.add))
                link(nc.vector.scalar_tensor_tensor(out=ln_a[:, :], in0=ln_a[:, :], scalar=0.25, in1=ln_a[:, :],
                                                    op0=ALU.mult, op1=ALU.mult))
                link(nc.vector.scalar_tensor_tensor(out=ln_b[:, :], in0=ln_b[:, :], scalar=1.0 / U,
                                                    in1=ln_a[:, :], op0=ALU.mult, op1=ALU.add))
                nc.vector.tensor_scalar(ln_b[:, :], ln_b[:, :], EPS, None, ALU.add).then_inc(variances, 1)
                ve.wait_ge(roots, i + 1)
                link(nc.vector.reciprocal(ln_r[:, :], ln_c[:, :]))
                link(nc.vector.tensor_scalar(ln_r[:, :], ln_r[:, :], factor, None, ALU.mult))
                link(nc.vector.scalar_tensor_tensor(out=ln_n[:, :], in0=ln_n[:, :], scalar=-0.5,
                                                    in1=ln_r[:, :], op0=ALU.mult, op1=ALU.mult))
                ve.sem_inc(scales, 1)

            def ln_piece(i):
                statistics(i, x_stage[:, i * LN_T:(i + 1) * LN_T, :], PART_SCALE, x_loaded, ln_steps,
                           ln_vars, ln_roots, ln_scales, h_full)

            def ln_low(i):
                ve.wait_ge(h_high, i + 1)
                s = slice(i * LN_T, (i + 1) * LN_T)
                nc.vector.tensor_tensor(h_lo[:, s, :], x_stage[:, s, :], h_hi[:, s, :], ALU.subtract)\
                  .then_inc(h_ready, 1)

            def check(rb, c):
                ve.wait_ge(f8_made, rb * CH + (c + 1))
                word = ring[:, c % SLOTS, :]
                nc.vector.scalar_tensor_tensor(out=word, in0=word, scalar=1.0, in1=word,
                                               op0=ALU.is_equal, op1=ALU.not_equal,
                                               accum_out=strays[:, bass.ds(rb * CH + c, 1)])\
                  .then_inc(chunk_checked, 1)

            def pack(stage, r, rb, g):
                src = f8ring[:, g % F8_SLOTS, :].bitcast(u32)
                done = rb * (3 * GR) + 3 * g

                def fold(to, high, low, shift, by):
                    nc.vector.scalar_tensor_tensor(out=to, in0=high, scalar=by, in1=low, op0=shift,
                                                   op1=ALU.bitwise_or).then_inc(pack_steps, 1)

                if not (isinstance(done, int) and done == 0):
                    ve.wait_ge(pack_steps, done)
                fold(folded[:, :], src[:, 4 * WORDS:], src[:, :4 * WORDS], ALU.logical_shift_right, 4)
                ve.wait_ge(pack_steps, done + 1)
                fold(folded[:, :2 * WORDS], folded[:, 2 * WORDS:], folded[:, :2 * WORDS], ALU.logical_shift_right, 2)
                ve.wait_ge(pack_steps, done + 2)
                fold(packed[:, packed_slot(g // 2, stage), g % 2, bass.ds(r, 1), :],
                     folded[:, WORDS:2 * WORDS], folded[:, :WORDS], ALU.logical_shift_left, 1)

            def unpack(unit, slot, free, k, n, r):
                ve.wait_ge(unit_used, free + START)
                src = packed[:, packed_slot(k, n), :, bass.ds(r, 1), :]
                for t in range(GT):
                    up = 4 * (t // 4) + 2 * (t // 2 % 2) - t % 2
                    shift = ALU.logical_shift_left if up >= 0 else ALU.logical_shift_right
                    last = nc.vector.tensor_scalar(unpacked[:, slot, t, :, :], src, abs(up), 0x40404040,
                                                   shift, ALU.bitwise_and)
                last.then_inc(unit_unpacked, 1)

            def bias(done, to, bank):
                ve.wait_ge(z_summed, done)
                nc.vector.tensor_tensor(as_tiles(to), as_tiles(bank),
                                        b_sb[:, None, :].broadcast_to([P, TPB, U]), ALU.add)\
                  .then_inc(z_biased, 1)

            def split_x1(done):
                ve.wait_ge(act_done, done)
                last = done - 1
                nc.vector.tensor_scalar(tiles(x1_hi, last), as_tiles(act[:, :]), PART_SCALE, None, ALU.mult,
                                        ALU.max, accum_out=tops[:, bass.ds(last, 1)]).then_inc(x1_high, 1)
                ve.wait_ge(x1_high, done)
                nc.vector.scalar_tensor_tensor(out=tiles(x1_lo, last), in0=as_tiles(act[:, :]),
                                               scalar=PART_SCALE, in1=tiles(x1_hi, last),
                                               op0=ALU.mult, op1=ALU.subtract).then_inc(x1_ready, 1)

            def row_block(stage, r):
                first = stage == 0 and isinstance(r, int)
                rb = r + RPS * stage
                units = units_of(stage)

                def unpacks(behind):
                    for u, (k, n) in enumerate(units):
                        if HALVES_AFTER[stage][2 * u] - 1 == behind:
                            index = r * len(units) + (UNIT_BASE[stage] + u)
                            unpack(index, unit_slot(u, stage), index if u == 0 else index - 1, k, n, r)

                if stage:
                    ve.wait_ge(pack_steps, 3 * GR * RPS * stage)
                unpacks(-1)
                if first:
                    ln_piece(0)
                    ln_low(0)
                for g in range(GR):
                    check(rb, 2 * g)
                    check(rb, 2 * g + 1)
                    pack(stage, r, rb, g)
                    if first and g % 2 == 1 and g < GR - 1:
                        ln_piece(g // 2 + 1)
                        ln_low(g // 2 + 1)
                    if g == 1 and not first:
                        bias(rb, act[:, :], bank_z[:, :])
                    if g == 2 and not first:
                        split_x1(rb)
                    unpacks(g)
                for m in range(stage - 1):
                    ve.wait_ge(unit_used, r * len(units) + (UNIT_BASE[stage] + stage + 1 + m + START))
                    ve.wait_ge(acc_copied, COPY_BASE[stage] + START)
                    ve.wait_ge(acc_added, ADD_BASE[stage] + START)
                    to = acc[:, bass.ds(r + RPS * m, 1), :].rearrange("p a n -> p (a n)")
                    nc.vector.scalar_tensor_tensor(out=to, in0=bank_sum[1 + m][:, :], scalar=UNSCALE,
                                                   in1=to, op0=ALU.mult, op1=ALU.add)\
                      .then_inc(acc_added, 1)

            for started in (z_biased, x1_ready, acc_added):
                ve.sem_inc(started, START)
            nc.vector.memset(ones[:, :], 1.0).then_inc(flag_steps, 1)
            stages(ve, row_block)
            bias(RB, act[:, :], bank_z[:, :])
            split_x1(RB)
            ve.wait_ge(pack_steps, 3 * GR * RB)

            def tail_unpack(t_units, unit, k, n, r):
                index = unit + UNIT_BASE[NS]
                unpack(index, unit_slot(t_units, NS), index - 1, k, n, r)

            def residual(e, t, n):
                ve.wait_ge(act_done, t + (RB + 1))
                ve.wait_ge(x_reloaded, 16)
                to = tiles(x_all, n)
                nc.vector.tensor_tensor(to, as_tiles(act_t[e % 2]), to, ALU.add)\
                  .then_inc(residual_added, 1)

            def tail_bias(e, t):
                bias(t + (RB + 1), act_t[e % 2], (bank_z if e % 2 == 0 else bank_first)[:, :])

            with ve.Fori(0, RPS // 2) as i:
                for e in range(2):
                    for k in range(NS):
                        tail_unpack(k, i * (2 * NS) + (e * NS + k), k, NS - 1, i * 2 + e)
                        if e == 1 and k == 1:
                            tail_bias(0, i * 2)
                        if e == 1 and k == 2:
                            residual(0, i * 2, i * 2 + (RB - RPS))
                tail_bias(1, i * 2 + 1)
                residual(1, i * 2 + 1, i * 2 + (RB - RPS + 1))

            def tail_sum(e, j):
                ve.wait_ge(unit_used, j + (UNIT_BASE[NS] + NS * RPS + 1 + START))
                ve.wait_ge(z_summed, j + (RB + RPS - 1))
                nc.vector.scalar_tensor_tensor(out=neigh_t[e % 2], in0=bank_sum[e % 2][:, :], scalar=UNSCALE,
                                               in1=acc[:, bass.ds(j, 1), :].rearrange("p a n -> p (a n)"),
                                               op0=ALU.mult, op1=ALU.add).then_inc(acc_added, 1)

            ve.wait_ge(acc_added, ADD_BASE[NS] + START)
            for m in range(NS - 1):
                ve.wait_ge(acc_copied, COPY_BASE[NS] + START)
                for e in range(RPS):
                    j = m * RPS + e
                    tail_unpack(j, RPS * NS + j, NS - 1, m, e)
                    if e >= 1:
                        tail_sum(e - 1, j - 1)
                    if e >= 2:
                        tail_bias(e - 2, j - 2 + RPS)
                        residual(e - 2, j - 2 + RPS, j - 2)
                tail_sum(3, m * RPS + 3)
                for e in (2, 3):
                    tail_bias(e, m * RPS + e + RPS)
                    residual(e, m * RPS + e + RPS, m * RPS + e)

            def step(n, instruction):
                instruction.then_inc(flag_steps, 1)
                ve.wait_ge(flag_steps, n + 1)

            step(1, nc.vector.tensor_scalar(tops[:, :], tops[:, :], LIMIT, None, ALU.is_gt, ALU.add,
                                            accum_out=found[:, 0:1]))
            step(2, nc.vector.tensor_scalar(strays[:, :], strays[:, :], 1.0, None, ALU.mult, ALU.add,
                                            accum_out=found[:, 1:2]))
            step(3, nc.vector.tensor_tensor(found[:, 2:3], found[:, 0:1], found[:, 1:2], ALU.add))
            ve.wait_ge(flag_summed, 1)
            nc.vector.tensor_scalar(flag[:, :], bank_flag[0:1, 0:1], 0.0, None, ALU.not_equal)\
              .then_inc(flag_ready, 1)

            ve.wait_ge(flag_ready, 1)
            general = ve.value_load(flag[0:1, 0:1], min_val=0, max_val=1)
            with ve.If(general == 1):
                ve.sem_inc(g_biased, START)
                for i in range(LN_PIECES):
                    statistics(i, g_h[:, i * LN_T:(i + 1) * LN_T, :], 1.0, g_x_loaded, g_ln_steps,
                               g_ln_vars, g_ln_roots, g_ln_scales, g_h_full)
                for rnd in range(2):
                    with ve.Fori(0, RB) as rb:
                        done = rb + rnd * RB
                        ve.wait_ge(g_z_summed, done + 1)
                        ve.wait_ge(g_swished, done + START)
                        nc.vector.tensor_tensor(as_tiles(g_act), as_tiles(bank_z[:, :]),
                                                b_sb[:, None, :].broadcast_to([P, TPB, U]), ALU.add)\
                          .then_inc(g_biased, 1)
                        if rnd:
                            ve.wait_ge(g_swished, done + (1 + START))
                            ve.wait_ge(g_x_reloaded, 16)
                            nc.vector.tensor_tensor(tiles(g_h, rb), as_tiles(g_act), tiles(g_h, rb),
                                                    ALU.add).then_inc(g_added, 1)

        @block.tensor
        def _(pe):
            def z_product(source, bank, summed=z_summed):
                for t in range(TPB):
                    last = nc.tensor.matmul(bank[:, t * U:(t + 1) * U], source[:, t * P:(t + 1) * P],
                                            w_sb[:, :], start=True, stop=True)
                last.then_inc(summed, 1)

            def unit_half(k, half, slot, bank, starts, ends):
                for t in range(GT):
                    tile = (2 * k + half) * GT + t
                    for part in (x1_hi, x1_lo):
                        last = nc.tensor.matmul(bank[:, :], part[:, tile, :], unit_tile(slot, half, t),
                                                start=starts and t == 0 and part is x1_hi,
                                                stop=ends and t == GT - 1 and part is x1_lo)
                return last

            def row_block(stage, r):
                first = stage == 0 and isinstance(r, int)
                rb = r + RPS * stage
                for g in range(GR):
                    for t in range(GT):
                        if t % TPC == 0:
                            pe.wait_ge(h_ready, g // 2 + 1)
                            if g == 0 and t == 0 and not first:
                                pe.wait_ge(neigh_copied, rb)
                            pe.wait_ge(f8_made, rb * CH + (2 * g + t // TPC + 1))
                            stand_alone(pe, tensor_passed)
                        for part in (h_hi, h_lo):
                            last = nc.tensor.matmul(bank_first[:, :], part[:, g * GT + t, :],
                                                    f8_tile(g % F8_SLOTS, t),
                                                    start=g == 0 and t == 0 and part is h_hi,
                                                    stop=g == GR - 1 and t == GT - 1 and part is h_lo)
                    last.then_inc(groups_done, 1)
                    if g == 0 and not first:
                        if stage == 0:
                            pe.wait_ge(w_loaded, 32)
                        pe.wait_ge(z_biased, rb - 1 + START)
                        z_product(neigh, bank_z)
                    for unit, half, starts, ends, s in halves_at(stage, g):
                        k = units_of(stage)[unit][0]
                        index = r * len(units_of(stage)) + (UNIT_BASE[stage] + unit)
                        if half == 0:
                            pe.wait_ge(x1_ready, (k + 1) * RPS + START)
                            pe.wait_ge(unit_unpacked, index + 1)
                            if starts and s == 0:
                                pe.wait_ge(acc_copied, r + (COPY_BASE[stage] + START))
                            if starts and s > 0:
                                pe.wait_ge(acc_added, r * (stage - 1) + (ADD_BASE[stage] + START))
                            stand_alone(pe, tensor_passed)
                        last = unit_half(k, half, unit_slot(unit, stage), bank_sum[s], starts, ends)
                        if half == 1:
                            last.then_inc(unit_used, 1)

            pe.sem_inc(unit_used, START)
            stages(pe, row_block)
            pe.wait_ge(neigh_copied, RB)
            pe.wait_ge(z_biased, RB - 1 + START)
            z_product(neigh, bank_z)

            def tail_unit(place, unit, k, bank, starts, ends, emptied=None, count=0):
                pe.wait_ge(x1_ready, (k + 1) * RPS + START)
                pe.wait_ge(unit_unpacked, unit + (UNIT_BASE[NS] + 1))
                if emptied is not None:
                    pe.wait_ge(emptied, count)
                stand_alone(pe, tensor_passed)
                for half in range(2):
                    last = unit_half(k, half, unit_slot(place, NS), bank, starts and half == 0,
                                     ends and half == 1)
                last.then_inc(unit_used, 1)

            def tail_z(e, t):
                pe.wait_ge(z_biased, t + (RB - 1 + START))
                z_product(neigh_t[e % 2], bank_z if e % 2 == 0 else bank_first)

            pe.wait_ge(acc_added, ADD_BASE[NS] + START)
            with pe.Fori(0, RPS // 2) as i:
                for e in range(2):
                    for k in range(NS):
                        tail_unit(k, i * (2 * NS) + (e * NS + k), k, bank_sum[e], k == 0, k == NS - 1,
                                  acc_copied if k == 0 else None, i * 2 + (COPY_BASE[NS] + e - 1 + START))
                        if e == 1 and k == 0:
                            pe.wait_ge(acc_copied, i * 2 + (COPY_BASE[NS] + 1 + START))
                            tail_z(0, i * 2)
                pe.wait_ge(acc_copied, i * 2 + (COPY_BASE[NS] + 2 + START))
                tail_z(1, i * 2 + 1)
            pe.wait_ge(acc_copied, COPY_BASE[NS] + RPS + START)
            with pe.Fori(0, (RB - RPS) // 4) as i:
                for e in range(4):
                    j = i * 4 + e
                    tail_unit(e, i * 4 + (NS * RPS + e), NS - 1, bank_sum[e % 2], True, True,
                              acc_added, j + (ADD_BASE[NS] - 1 + START))
                    if e:
                        pe.wait_ge(acc_added, j + (ADD_BASE[NS] + START))
                        tail_z(e - 1, i * 4 + (e - 1 + RPS))
                pe.wait_ge(acc_added, i * 4 + (ADD_BASE[NS] + 4 + START))
                tail_z(3, i * 4 + (3 + RPS))

            pe.wait_ge(flag_steps, 4)
            nc.tensor.matmul(bank_flag[0:1, 0:1], found[:, 2:3], ones[:, :], start=True, stop=True)\
              .then_inc(flag_summed, 1)

            pe.wait_ge(flag_ready, 1)
            general = pe.value_load(flag[0:1, 0:1], min_val=0, max_val=1)
            with pe.If(general == 1):
                pe.sem_inc(g_chunk_used, SLOTS)
                for rnd in range(2):
                    source = g_x1 if rnd else g_h
                    with pe.Fori(0, RB) as rb:
                        done = rb + rnd * RB
                        pe.wait_ge(g_h_full, LN_PIECES)
                        if rnd:
                            pe.wait_ge(g_swished, RB + START)
                        pe.wait_ge(g_copied, done + START)
                        for c in range(CH):
                            pe.wait_ge(g_chunk_loaded[c % SLOTS],
                                       rb * (16 * CH // SLOTS) + 16 * (rnd * RB * CH // SLOTS + c // SLOTS + 1))
                            for t in range(TPC):
                                last = nc.tensor.matmul(bank_first[:, :], source[:, c * TPC + t, :],
                                                        ring[:, c % SLOTS, t * NB:(t + 1) * NB],
                                                        start=c == 0 and t == 0,
                                                        stop=c == CH - 1 and t == TPC - 1)
                            last.then_inc(g_chunk_used, 1)
                        pe.wait_ge(g_copied, done + (1 + START))
                        pe.wait_ge(g_biased, done + START)
                        z_product(neigh, bank_z, g_z_summed)


def kernel(x, adj, L0_gnn_W, L0_gnn_b):
    import numpy as np
    import concourse.bacc as bacc
    from concourse.bass_utils import run_bass_kernel_spmd

    x, w, b = (np.ascontiguousarray(a) for a in (x, L0_gnn_W, L0_gnn_b))
    blocks = np.asarray(adj).reshape(P, RB, TPB, P, CH, TPC).transpose(1, 4, 3, 5, 2, 0)
    adj_blocks = np.ascontiguousarray(blocks).reshape(RB, CH, P, CHUNK)

    nc = bacc.Bacc("TRN2", target_bir_lowering=False, num_devices=1)
    arrays = {"x_dram": x, "adj_dram": adj_blocks, "w_dram": w, "b_dram": b}
    args = [nc.dram_tensor(name, a.shape, mybir.dt.from_np(a.dtype), kind="ExternalInput").ap()
            for name, a in arrays.items()]
    out = nc.dram_tensor("out_dram", x.shape, mybir.dt.float32, kind="ExternalOutput").ap()
    graph_block(nc, *args, out)
    r = run_bass_kernel_spmd(nc, [arrays], core_ids=[0])
    return r.results[0]["out_dram"]
```

```python
from contextlib import ExitStack

import concourse.bass as bass
from concourse import mybir

P = 128
N = 8192
U = 128
KT = N // P
NB = 512
RB = N // NB
TPB = NB // P
TPC = 4
CHUNK = TPC * NB
CH = KT // TPC
GT = 8
GR = KT // GT
SLOTS = 4
F8_SLOTS = 4
NS = 4
RPS = RB // NS
WORDS = NB // 4
ONE8 = 2.0
PART_SCALE = 256.0
UNSCALE = 1.0 / (ONE8 * PART_SCALE)
LIMIT = 32768.0 / PART_SCALE
EPS = 1e-5
START = 1
LN_PIECES = 4
LN_T = KT // LN_PIECES

HALVES_AFTER = {0: [], 1: [2, 5], 2: [0, 1, 3, 4, 5, 6], 3: [0, 1, 2, 3, 3, 4, 5, 6, 6, 7]}


def sums_of(stage):
    if stage == 0:
        return []
    return [[(k, stage - 1) for k in range(stage)]] + [[(stage - 1, n)] for n in range(stage - 1)]


def units_of(stage):
    return [unit for one in sums_of(stage) for unit in one]


UNIT_BASE = [RPS * sum(len(units_of(s)) for s in range(stage)) for stage in range(NS + 1)]
COPY_BASE = [RPS * max(stage - 1, 0) for stage in range(NS + 1)]
TAIL_UNITS = NS * RPS + (RB - RPS)


def tail_unit(u):
    return divmod(u, NS) if u < NS * RPS else (RPS + u - NS * RPS, NS - 1)


ADD_BASE = [RPS * sum(max(s - 1, 0) for s in range(stage)) for stage in range(NS + 1)]


def packed_slot(k, n):
    if n < NS - 1:
        return n * NS + k
    return [packed_slot(0, 0), packed_slot(1, 0), packed_slot(0, 1), packed_slot(1, 1)][k]


def graph_block(nc, x, adj, w, b, out):
    f32, f16, f8 = mybir.dt.float32, mybir.dt.float16, mybir.dt.float8e4
    u32 = mybir.dt.uint32
    ALU = mybir.AluOpType
    ACT = mybir.ActivationFunctionType
    AX = mybir.AxisListType

    x_v = x.rearrange("(p t) u -> p t u", t=KT)
    out_v = out.rearrange("(p t) u -> p t u", t=KT)

    ctx = ExitStack()
    with ctx:
        def sb(name, shape, dt):
            return ctx.enter_context(nc.sbuf_tensor(name, shape, dt))

        def pb(name):
            return ctx.enter_context(nc.psum_tensor(name, [P, NB], f32))

        def sem(name):
            return ctx.enter_context(nc.semaphore(name))

        ring = sb("adj_ring", [P, SLOTS, CHUNK], f32)
        x_all = ring[:, :, :].rearrange("p s (t u) -> p (s t) u", u=U)
        f8ring = sb("f8_ring", [P, F8_SLOTS, GT * NB], f8)
        packed = sb("packed", [P, 12, 2, RPS, WORDS], u32)
        x_stage = packed[:, 4:12].rearrange("p a b c w -> p (a b c w)").bitcast(f32)\
            .rearrange("p (t u) -> p t u", u=U)
        h_parts = sb("h_parts", [P, 2, KT, U], f16)
        h_hi, h_lo = h_parts[:, 0], h_parts[:, 1]
        x1_parts = sb("x1_parts", [P, 2, KT, U], f16)
        x1_hi, x1_lo = x1_parts[:, 0], x1_parts[:, 1]
        acc = sb("acc", [P, RB - RPS, NB], f32)
        unpacked = sb("unpacked", [P, 2, GT, 2, WORDS], u32)
        folded = sb("folded", [P, 4 * WORDS], u32)
        folded_twice = sb("folded_twice", [P, 2 * WORDS], u32)
        w_sb = sb("w_sb", [P, U], f32)
        b_sb = sb("b_sb", [P, U], f32)
        neigh = sb("neigh", [P, NB], f32)
        act = neigh
        ln_space = unpacked[:, 0].rearrange("p t h w -> p (t h w)").bitcast(f32)
        stats = ln_space[:, 0:6 * KT].rearrange("p (t s) -> p t s", s=6)
        ln_a, ln_b, ln_c, ln_r, ln_n = (ln_space[:, (6 + i) * KT:(7 + i) * KT] for i in range(5))
        strays = sb("strays", [P, RB * CH], f32)
        tops = sb("tops", [P, 1], f32)
        found = sb("found", [P, 4], f32)
        ones = sb("ones", [P, 1], f32)
        flag = sb("flag", [1, 1], u32)
        neigh_t = [f8ring[:, i].bitcast(f32)[:, 0:NB] for i in range(2)]
        act_t = [f8ring[:, 2 + i].bitcast(f32)[:, 0:NB] for i in range(2)]

        g_h = h_parts[:, :, :, :].rearrange("p a t u -> p (a t u)").bitcast(f32)\
            .rearrange("p (t u) -> p t u", u=U)
        g_x1 = x1_parts[:, :, :, :].rearrange("p a t u -> p (a t u)").bitcast(f32)\
            .rearrange("p (t u) -> p t u", u=U)
        g_act = act_t[0]

        bank_first = pb("bank_first")
        bank_z = pb("bank_z")
        bank_sum = [pb(f"bank_sum{i}") for i in range(3)]
        bank_flag = pb("bank_flag")

        x_loaded = [sem(f"x_loaded{i}") for i in range(LN_PIECES)]
        w_loaded = sem("w_loaded")
        chunk_loaded = [sem(f"chunk_loaded{i}") for i in range(SLOTS)]
        f8_made = sem("f8_made")
        chunk_checked = sem("chunk_checked")
        pack_steps = sem("pack_steps")
        ln_steps = sem("ln_steps")
        ln_vars = sem("ln_vars")
        ln_roots = sem("ln_roots")
        ln_scales = sem("ln_scales")
        h_scaled = sem("h_scaled")
        h_fp32 = sem("h_fp32")
        h_high = sem("h_high")
        h_ready = sem("h_ready")
        groups_done = sem("groups_done")
        neigh_copied = sem("neigh_copied")
        z_summed = sem("z_summed")
        z_biased = sem("z_biased")
        act_done = sem("act_done")
        x1_high = sem("x1_high")
        x1_widened = sem("x1_widened")
        x1_ready = sem("x1_ready")
        unit_unpacked = sem("unit_unpacked")
        unit_used = sem("unit_used")
        acc_copied = sem("acc_copied")
        acc_added = sem("acc_added")
        residual_added = sem("residual_added")
        x_reloaded = sem("x_reloaded")
        out_stored = sem("out_stored")
        scalar_passed = sem("scalar_passed")
        tensor_passed = sem("tensor_passed")
        vector_passed = sem("vector_passed")
        pool_passed = sem("pool_passed")
        flag_steps = sem("flag_steps")
        flag_summed = sem("flag_summed")
        flag_ready = sem("flag_ready")

        g_x_loaded = [sem(f"g_x_loaded{i}") for i in range(LN_PIECES)]
        g_ln_steps = sem("g_ln_steps")
        g_ln_vars = sem("g_ln_vars")
        g_ln_roots = sem("g_ln_roots")
        g_ln_scales = sem("g_ln_scales")
        g_h_scaled = sem("g_h_scaled")
        g_h_ready = sem("g_h_ready")
        g_chunk_loaded = [sem(f"g_chunk_loaded{i}") for i in range(SLOTS)]
        g_chunk_used = sem("g_chunk_used")
        g_copied = sem("g_copied")
        g_biased = sem("g_biased")
        g_swished = sem("g_swished")
        g_z_summed = sem("g_z_summed")
        g_x_reloaded = sem("g_x_reloaded")
        g_added = sem("g_added")
        g_stored = sem("g_stored")

        def f8_tile(group_slot, t):
            return f8ring[:, group_slot, t * NB:(t + 1) * NB]

        def unit_tile(slot, half, t):
            return unpacked[:, slot, t, half, :].bitcast(f8)

        def tiles(buf, rb):
            return buf[:, bass.ds(rb * TPB, TPB), :]

        def as_tiles(buf):
            return buf.rearrange("p (t u) -> p t u", u=U)

        def stand_alone(eng, passed):
            eng.sem_inc(passed, 1)

        def unit_slot(unit_in_stage, stage):
            return unit_in_stage % 2 if stage < NS else (unit_in_stage + 1) % 2

        def halves_at(stage, group):
            found_halves = []
            where = [(s, i, len(one)) for s, one in enumerate(sums_of(stage)) for i in range(len(one))]
            for q, g in enumerate(HALVES_AFTER[stage]):
                if g == group:
                    s, i, n = where[q // 2]
                    found_halves.append((q // 2, q % 2, i == 0 and q % 2 == 0, i == n - 1 and q % 2 == 1, s))
            return found_halves

        def stages(eng, body):
            body(0, 0)
            with eng.Fori(1, RPS) as r:
                body(0, r)
            for stage in range(1, NS):
                with eng.Fori(0, RPS) as r:
                    body(stage, r)

        block = ctx.enter_context(nc.Block())

        @block.sync
        def _(sp):
            for i in range(LN_PIECES):
                sp.dma_start(x_stage[:, i * LN_T:(i + 1) * LN_T, :],
                             x_v[:, i * LN_T:(i + 1) * LN_T, :]).then_inc(x_loaded[i], 16)
                if i == LN_PIECES // 2:
                    sp.dma_start(ring[:, 0, :], adj[0, 0]).then_inc(chunk_loaded[0], 16)
            sp.dma_start(ring[:, 1, :], adj[0, 1]).then_inc(chunk_loaded[1], 16)
            sp.dma_start(w_sb[:, :], w).then_inc(w_loaded, 16)
            sp.dma_start(b_sb[:, :], b.partition_broadcast(P)).then_inc(w_loaded, 16)

            def loads(stage, r):
                first = stage == 0 and isinstance(r, int)
                rb = r + RPS * stage
                for c in range(CH):
                    if first and c < 2:
                        continue
                    if not (first and c < SLOTS):
                        sp.wait_ge(chunk_checked, rb * CH + (c - SLOTS + 1))
                    sp.dma_start(ring[:, c % SLOTS, :], adj[rb, c]).then_inc(chunk_loaded[c % SLOTS], 16)

            stages(sp, loads)
            sp.wait_ge(chunk_checked, RB * CH)
            sp.dma_start(x_all, x_v).then_inc(x_reloaded, 16)

            for t in range(RB):
                sp.wait_ge(residual_added, t + 1)
                sp.dma_start(tiles(out_v, RB - 1 - t), tiles(x_all, RB - 1 - t)).then_inc(out_stored, 16)
            sp.wait_ge(out_stored, 16 * RB)

            sp.wait_ge(flag_ready, 1)
            general = sp.value_load(flag[0:1, 0:1], min_val=0, max_val=1)
            with sp.If(general == 1):
                for i in range(LN_PIECES):
                    s = slice(i * LN_T, (i + 1) * LN_T)
                    sp.dma_start(g_h[:, s, :], x_v[:, s, :]).then_inc(g_x_loaded[i], 16)
                for rnd in range(2):
                    with sp.Fori(0, RB) as rb:
                        for c in range(CH):
                            sp.wait_ge(g_chunk_used, rb * CH + (rnd * RB * CH + c + 1))
                            sp.dma_start(ring[:, c % SLOTS, :], adj[rb, c])\
                              .then_inc(g_chunk_loaded[c % SLOTS], 16)
                    if rnd == 0:
                        sp.wait_ge(g_chunk_used, RB * CH + SLOTS)
                        sp.dma_start(g_h, x_v).then_inc(g_x_reloaded, 16)

        @block.scalar
        def _(sc):
            def ln_root(variances, roots):
                sc.wait_ge(variances, 1)
                nc.scalar.activation(ln_c, ln_b, ACT.Sqrt).then_inc(roots, 1)

            def high_part(i):
                s = slice(i * LN_T, (i + 1) * LN_T)
                if i % 2:
                    sc.wait_ge(ln_scales, 1)
                    for t in range(i * LN_T, (i + 1) * LN_T):
                        row = x_stage[:, t, :]
                        last = nc.scalar.activation(row, row, ACT.Relu, bias=ln_n[:, t:t + 1],
                                                    scale=ln_r[:, t:t + 1])
                else:
                    sc.wait_ge(h_scaled, i // 2 + 1)
                    last = nc.scalar.activation(x_stage[:, s, :], x_stage[:, s, :], ACT.Relu)
                last.then_inc(h_fp32, 1)
                sc.wait_ge(h_fp32, i + 1)
                nc.scalar.activation(h_hi[:, s, :], x_stage[:, s, :], ACT.Copy).then_inc(h_high, 1)

            def copy_neigh(done):
                sc.wait_ge(groups_done, done * GR)
                sc.wait_ge(x1_ready, done - 1 + START)
                nc.scalar.activation(neigh[:, :], bank_first[:, :], ACT.Copy, scale=UNSCALE)\
                  .then_inc(neigh_copied, 1)

            def swish(done):
                sc.wait_ge(z_biased, done + START)
                nc.scalar.activation(act[:, :], act[:, :], ACT.Silu).then_inc(act_done, 1)
                sc.wait_ge(act_done, done)
                nc.scalar.activation(tiles(x1_hi, done - 1), as_tiles(act[:, :]), ACT.Copy,
                                     scale=PART_SCALE).then_inc(x1_high, 1)

            def row_block(stage, r):
                first = stage == 0 and isinstance(r, int)
                rb = r + RPS * stage
                for g in range(GR):
                    if first and g == 0:
                        ln_root(ln_vars, ln_roots)
                    for half in range(2):
                        c = 2 * g + half
                        if half == 0 and not (first and g < F8_SLOTS):
                            sc.wait_ge(groups_done, rb * GR + (g - F8_SLOTS + 1))
                            sc.wait_ge(pack_steps, rb * (3 * GR) + (3 * (g - F8_SLOTS) + 1))
                        sc.wait_ge(chunk_loaded[c % SLOTS], rb * (16 * CH // SLOTS) + 16 * (c // SLOTS + 1))
                        stand_alone(sc, scalar_passed)
                        nc.scalar.activation(f8ring[:, g % F8_SLOTS, half * CHUNK:(half + 1) * CHUNK],
                                             ring[:, c % SLOTS, :], ACT.Copy, scale=ONE8,
                                             saturate=False).then_inc(f8_made, 1)
                    if first and g < LN_PIECES:
                        high_part(g)
                    if g == 0 and not first:
                        copy_neigh(rb)
                    if g == 2 and not first:
                        swish(rb)
                if stage:
                    sc.wait_ge(unit_used, r * len(units_of(stage)) + (UNIT_BASE[stage] + stage + START))
                    nc.scalar.activation(acc[:, bass.ds(r + RPS * (stage - 1), 1), :], bank_sum[0][:, :],
                                         ACT.Copy, scale=UNSCALE).then_inc(acc_copied, 1)

            sc.sem_inc(acc_copied, START)
            stages(sc, row_block)
            copy_neigh(RB)
            swish(RB)

            for t in range(RB):
                if t < RPS:
                    sc.wait_ge(unit_used, UNIT_BASE[NS] + NS * (t + 1) + START)
                    sc.wait_ge(z_summed, RB + t - 1)
                    nc.scalar.activation(neigh_t[t % 2], bank_sum[t % 2][:, :], ACT.Copy, scale=UNSCALE)\
                      .then_inc(acc_copied, 1)
                sc.wait_ge(z_biased, RB + t + 1 + START)
                nc.scalar.activation(act_t[t % 2], act_t[t % 2], ACT.Silu).then_inc(act_done, 1)

            sc.wait_ge(flag_ready, 1)
            general = sc.value_load(flag[0:1, 0:1], min_val=0, max_val=1)
            with sc.If(general == 1):
                sc.sem_inc(g_copied, START)
                sc.sem_inc(g_swished, START)
                ln_root(g_ln_vars, g_ln_roots)
                for i in range(LN_PIECES):
                    part = g_h[:, i * LN_T:(i + 1) * LN_T, :]
                    sc.wait_ge(g_h_scaled, i + 1)
                    nc.scalar.activation(part, part, ACT.Relu).then_inc(g_h_ready, 1)
                for rnd in range(2):
                    with sc.Fori(0, RB) as rb:
                        done = rb + rnd * RB
                        sc.wait_ge(g_chunk_used, rb * CH + ((rnd * RB + 1) * CH + SLOTS))
                        nc.scalar.activation(neigh[:, :], bank_first[:, :], ACT.Copy).then_inc(g_copied, 1)
                        sc.wait_ge(g_biased, done + (1 + START))
                        to = as_tiles(g_act) if rnd else tiles(g_x1, rb)
                        nc.scalar.activation(to, as_tiles(g_act), ACT.Silu).then_inc(g_swished, 1)
                        if rnd:
                            sc.wait_ge(g_added, rb + 1)
                            sc.dma_start(tiles(out_v, rb), tiles(g_h, rb)).then_inc(g_stored, 16)
                sc.wait_ge(g_stored, 16 * RB)

        @block.gpsimd
        def _(po):
            def scale_rows(part_of, i, scaled):
                for t in range(i * LN_T, (i + 1) * LN_T):
                    row = part_of[:, t, :]
                    last = nc.gpsimd.tensor_scalar(row, row, ln_r[:, t:t + 1], ln_n[:, t:t + 1],
                                                   ALU.mult, ALU.add)
                last.then_inc(scaled, 1)

            def low_part(i):
                po.wait_ge(h_high, i + 1)
                s = slice(i * LN_T, (i + 1) * LN_T)
                nc.gpsimd.tensor_tensor(h_lo[:, s, :], x_stage[:, s, :], h_hi[:, s, :], ALU.subtract)\
                  .then_inc(h_ready, 1)

            def low_x1(done):
                po.wait_ge(x1_high, done)
                stand_alone(po, pool_passed)
                nc.gpsimd.tensor_scalar(act[:, :], act[:, :], PART_SCALE, None, ALU.mult)\
                  .then_inc(x1_widened, 1)
                po.wait_ge(x1_widened, done)
                nc.gpsimd.tensor_tensor(tiles(x1_lo, done - 1), as_tiles(act[:, :]),
                                        tiles(x1_hi, done - 1), ALU.subtract).then_inc(x1_ready, 1)

            po.sem_inc(x1_ready, START)
            po.wait_ge(ln_scales, 1)
            scale_rows(x_stage, 0, h_scaled)
            for i in range(LN_PIECES):
                if i + 1 < LN_PIECES and (i + 1) % 2 == 0:
                    scale_rows(x_stage, i + 1, h_scaled)
                low_part(i)
            with po.Fori(1, RB + 1) as done:
                low_x1(done)

            po.wait_ge(flag_ready, 1)
            general = po.value_load(flag[0:1, 0:1], min_val=0, max_val=1)
            with po.If(general == 1):
                po.wait_ge(g_ln_scales, 1)
                for i in range(LN_PIECES):
                    scale_rows(g_h, i, g_h_scaled)

        @block.vector
        def _(ve):
            def statistics(source, factor, loaded, counted, variances, roots, scales):
                steps = [0]

                def link(instruction):
                    instruction.then_inc(counted, 1)
                    steps[0] += 1
                    ve.wait_ge(counted, steps[0])

                for t in range(KT):
                    if t % LN_T == 0:
                        ve.wait_ge(loaded[t // LN_T], 16)
                    last = nc.vector.bn_stats(stats[:, t, :], source[:, t, :])
                link(last)
                nc.vector.tensor_tensor(ln_a, stats[:, :, 1], stats[:, :, 4], ALU.subtract)
                nc.vector.tensor_tensor(ln_n, stats[:, :, 1], stats[:, :, 4], ALU.add)
                link(nc.vector.tensor_tensor(ln_b, stats[:, :, 2], stats[:, :, 5], ALU.add))
                link(nc.vector.scalar_tensor_tensor(out=ln_a, in0=ln_a, scalar=0.25, in1=ln_a,
                                                    op0=ALU.mult, op1=ALU.mult))
                link(nc.vector.scalar_tensor_tensor(out=ln_b, in0=ln_b, scalar=1.0 / U, in1=ln_a,
                                                    op0=ALU.mult, op1=ALU.add))
                nc.vector.tensor_scalar(ln_b, ln_b, EPS, None, ALU.add).then_inc(variances, 1)
                ve.wait_ge(roots, 1)
                link(nc.vector.reciprocal(ln_r, ln_c))
                link(nc.vector.tensor_scalar(ln_r, ln_r, factor, None, ALU.mult))
                nc.vector.scalar_tensor_tensor(out=ln_n, in0=ln_n, scalar=-0.5, in1=ln_r,
                                               op0=ALU.mult, op1=ALU.mult).then_inc(scales, 1)

            def check(rb, c):
                ve.wait_ge(f8_made, rb * CH + (c + 1))
                word = ring[:, c % SLOTS, :]
                nc.vector.scalar_tensor_tensor(out=word, in0=word, scalar=1.0, in1=word,
                                               op0=ALU.is_equal, op1=ALU.not_equal,
                                               accum_out=strays[:, bass.ds(rb * CH + c, 1)])\
                  .then_inc(chunk_checked, 1)

            def fold(to, high, low, shift, by):
                nc.vector.scalar_tensor_tensor(out=to, in0=high, scalar=by, in1=low, op0=shift,
                                               op1=ALU.bitwise_or).then_inc(pack_steps, 1)

            def pack_1(rb, g):
                src = f8ring[:, g % F8_SLOTS, :].bitcast(u32)
                done = rb * (3 * GR) + 3 * g
                if not isinstance(done, int):
                    ve.wait_ge(pack_steps, done - 1)
                elif done:
                    ve.wait_ge(pack_steps, done - 1)
                fold(folded[:, :], src[:, 4 * WORDS:], src[:, :4 * WORDS], ALU.logical_shift_right, 4)

            def pack_2(rb, g):
                ve.wait_ge(pack_steps, rb * (3 * GR) + (3 * g + 1))
                fold(folded_twice[:, :], folded[:, 2 * WORDS:], folded[:, :2 * WORDS],
                     ALU.logical_shift_right, 2)

            def pack_3(stage, r, rb, g):
                ve.wait_ge(pack_steps, rb * (3 * GR) + (3 * g + 2))
                fold(packed[:, packed_slot(g // 2, stage), g % 2, bass.ds(r, 1), :],
                     folded_twice[:, WORDS:], folded_twice[:, :WORDS], ALU.logical_shift_left, 1)

            def unpack(unit, slot, free, k, n, r):
                ve.wait_ge(unit_used, free + START)
                src = packed[:, packed_slot(k, n), :, bass.ds(r, 1), :]
                for t in range(GT):
                    up = 4 * (t // 4) + 2 * (t // 2 % 2) - t % 2
                    shift = ALU.logical_shift_left if up >= 0 else ALU.logical_shift_right
                    last = nc.vector.tensor_scalar(unpacked[:, slot, t, :, :], src, abs(up), 0x40404040,
                                                   shift, ALU.bitwise_and)
                last.then_inc(unit_unpacked, 1)

            def bias_x1(done):
                ve.wait_ge(z_summed, done)
                ve.wait_ge(z_biased, done - 1 + START)
                stand_alone(ve, vector_passed)
                nc.vector.tensor_tensor_reduce(out=as_tiles(act[:, :]), in0=as_tiles(bank_z[:, :]),
                                               in1=b_sb[:, None, :].broadcast_to([P, TPB, U]), scale=1.0,
                                               scalar=tops[:, :], op0=ALU.add, op1=ALU.max,
                                               accum_out=tops[:, :]).then_inc(z_biased, 1)

            def bias(done, to, bank):
                ve.wait_ge(z_summed, done)
                nc.vector.tensor_tensor(as_tiles(to), as_tiles(bank),
                                        b_sb[:, None, :].broadcast_to([P, TPB, U]), ALU.add)\
                  .then_inc(z_biased, 1)

            def add_sum(stage, r, m):
                ve.wait_ge(unit_used, r * len(units_of(stage)) + (UNIT_BASE[stage] + stage + 1 + m + START))
                ve.wait_ge(acc_copied, COPY_BASE[stage] + START)
                ve.wait_ge(acc_added, ADD_BASE[stage] + START)
                to = acc[:, bass.ds(r + RPS * m, 1), :].rearrange("p a n -> p (a n)")
                nc.vector.scalar_tensor_tensor(out=to, in0=bank_sum[1 + m][:, :], scalar=UNSCALE,
                                               in1=to, op0=ALU.mult, op1=ALU.add)\
                  .then_inc(acc_added, 1)

            def row_block(stage, r):
                first = stage == 0 and isinstance(r, int)
                rb = r + RPS * stage
                units = units_of(stage)

                def unpacks(behind):
                    for u, (k, n) in enumerate(units):
                        if HALVES_AFTER[stage][2 * u] - 1 == behind:
                            index = r * len(units) + (UNIT_BASE[stage] + u)
                            unpack(index, unit_slot(u, stage), index if u == 0 else index - 1, k, n, r)

                if stage:
                    ve.wait_ge(pack_steps, 3 * GR * RPS * stage)
                unpacks(-1)
                if first:
                    statistics(x_stage, PART_SCALE, x_loaded, ln_steps, ln_vars, ln_roots, ln_scales)
                for g in range(GR):
                    check(rb, 2 * g)
                    if g:
                        pack_2(rb, g - 1)
                    check(rb, 2 * g + 1)
                    if g:
                        pack_3(stage, r, rb, g - 1)
                    pack_1(rb, g)
                    if g == 1 and not first:
                        bias_x1(rb)
                    unpacks(g)
                sums = list(range(stage - 1))
                for m in sums[:1]:
                    add_sum(stage, r, m)
                pack_2(rb, GR - 1)
                for m in sums[1:]:
                    add_sum(stage, r, m)
                pack_3(stage, r, rb, GR - 1)

            for started in (z_biased, acc_added):
                ve.sem_inc(started, START)
            nc.vector.memset(ones[:, :], 1.0)
            nc.vector.memset(tops[:, :], 0.0).then_inc(flag_steps, 1)
            ve.wait_ge(flag_steps, 1)
            stages(ve, row_block)
            ve.wait_ge(pack_steps, 3 * GR * RB)
            ve.wait_ge(acc_copied, COPY_BASE[NS] + START)
            ve.wait_ge(acc_added, ADD_BASE[NS] + START)

            def tail_unpack(u):
                t, k = tail_unit(u)
                n = RB - 1 - t
                index = UNIT_BASE[NS] + u
                unpack(index, unit_slot(u, NS), index - 1, k, n // RPS, n % RPS)

            def tail_sum(t):
                ve.wait_ge(unit_used, UNIT_BASE[NS] + RPS * NS + (t - RPS + 1) + START)
                ve.wait_ge(z_summed, RB + t - 1)
                nc.vector.scalar_tensor_tensor(out=neigh_t[t % 2], in0=bank_sum[t % 2][:, :], scalar=UNSCALE,
                                               in1=acc[:, RB - 1 - t, :],
                                               op0=ALU.mult, op1=ALU.add).then_inc(acc_added, 1)

            def tail_bias(t):
                bias(RB + t + 1, act_t[t % 2], (bank_first if t % 2 else bank_z)[:, :])

            def residual(t):
                ve.wait_ge(act_done, RB + t + 1)
                ve.wait_ge(x_reloaded, 16)
                to = tiles(x_all, RB - 1 - t)
                nc.vector.tensor_tensor(to, as_tiles(act_t[t % 2]), to, ALU.add)\
                  .then_inc(residual_added, 1)

            tail_unpack(0)
            bias_x1(RB)
            tail_unpack(1)
            def step(n, instruction):
                instruction.then_inc(flag_steps, 1)
                ve.wait_ge(flag_steps, n + 1)

            ve.wait_ge(z_biased, RB + START)
            ve.wait_ge(chunk_checked, RB * CH)
            step(1, nc.vector.tensor_scalar(found[:, 0:1], tops[:, :], LIMIT, None, ALU.is_gt))
            step(2, nc.vector.tensor_scalar(strays[:, :], strays[:, :], 1.0, None, ALU.mult, ALU.add,
                                            accum_out=found[:, 1:2]))
            step(3, nc.vector.tensor_tensor(found[:, 2:3], found[:, 0:1], found[:, 1:2], ALU.add))

            for t in range(RPS):
                tail_unpack(NS * t + 2)
                if t:
                    tail_bias(t - 1)
                tail_unpack(NS * t + 3)
                if t:
                    residual(t - 1)
                tail_unpack(NS * t + 4)
                if t < RPS - 1:
                    tail_unpack(NS * t + 5)
            ve.wait_ge(flag_summed, 1)
            nc.vector.tensor_scalar(flag[:, :], bank_flag[0:1, 0:1], 0.0, None, ALU.not_equal)\
              .then_inc(flag_ready, 1)

            for t in range(RPS, RB):
                if NS * RPS + (t - RPS) + 1 < TAIL_UNITS:
                    tail_unpack(NS * RPS + (t - RPS) + 1)
                if t == RPS:
                    tail_bias(t - 1)
                    residual(t - 1)
                tail_sum(t)
                if t > RPS:
                    tail_bias(t - 1)
                    residual(t - 1)
            tail_bias(RB - 1)
            residual(RB - 1)

            ve.wait_ge(flag_ready, 1)
            general = ve.value_load(flag[0:1, 0:1], min_val=0, max_val=1)
            with ve.If(general == 1):
                ve.sem_inc(g_biased, START)
                statistics(g_h, 1.0, g_x_loaded, g_ln_steps, g_ln_vars, g_ln_roots, g_ln_scales)
                for rnd in range(2):
                    with ve.Fori(0, RB) as rb:
                        done = rb + rnd * RB
                        ve.wait_ge(g_z_summed, done + 1)
                        ve.wait_ge(g_swished, done + START)
                        nc.vector.tensor_tensor(as_tiles(g_act), as_tiles(bank_z[:, :]),
                                                b_sb[:, None, :].broadcast_to([P, TPB, U]), ALU.add)\
                          .then_inc(g_biased, 1)
                        if rnd:
                            ve.wait_ge(g_swished, done + (1 + START))
                            ve.wait_ge(g_x_reloaded, 16)
                            nc.vector.tensor_tensor(tiles(g_h, rb), as_tiles(g_act), tiles(g_h, rb),
                                                    ALU.add).then_inc(g_added, 1)

        @block.tensor
        def _(pe):
            def z_product(source, bank, summed=z_summed):
                for t in range(TPB):
                    last = nc.tensor.matmul(bank[:, t * U:(t + 1) * U], source[:, t * P:(t + 1) * P],
                                            w_sb[:, :], start=True, stop=True)
                last.then_inc(summed, 1)

            def unit_half(k, half, slot, bank, starts, ends):
                for t in range(GT):
                    tile = (2 * k + half) * GT + t
                    for part in (x1_hi, x1_lo):
                        last = nc.tensor.matmul(bank[:, :], part[:, tile, :], unit_tile(slot, half, t),
                                                start=starts and t == 0 and part is x1_hi,
                                                stop=ends and t == GT - 1 and part is x1_lo)
                return last

            def row_block(stage, r):
                first = stage == 0 and isinstance(r, int)
                rb = r + RPS * stage
                for g in range(GR):
                    for t in range(GT):
                        if t % TPC == 0:
                            pe.wait_ge(h_ready, g // 2 + 1)
                            if g == 0 and t == 0 and not first:
                                pe.wait_ge(neigh_copied, rb)
                            pe.wait_ge(f8_made, rb * CH + (2 * g + t // TPC + 1))
                            stand_alone(pe, tensor_passed)
                        for part in (h_hi, h_lo):
                            last = nc.tensor.matmul(bank_first[:, :], part[:, g * GT + t, :],
                                                    f8_tile(g % F8_SLOTS, t),
                                                    start=g == 0 and t == 0 and part is h_hi,
                                                    stop=g == GR - 1 and t == GT - 1 and part is h_lo)
                    last.then_inc(groups_done, 1)
                    if g == 0 and not first:
                        if stage == 0:
                            pe.wait_ge(w_loaded, 32)
                        pe.wait_ge(z_biased, rb - 1 + START)
                        z_product(neigh, bank_z)
                    for unit, half, starts, ends, s in halves_at(stage, g):
                        k = units_of(stage)[unit][0]
                        index = r * len(units_of(stage)) + (UNIT_BASE[stage] + unit)
                        if half == 0:
                            pe.wait_ge(x1_ready, (k + 1) * RPS + START)
                            pe.wait_ge(unit_unpacked, index + 1)
                            if starts and s == 0:
                                pe.wait_ge(acc_copied, r + (COPY_BASE[stage] + START))
                            if starts and s > 0:
                                pe.wait_ge(acc_added, r * (stage - 1) + (ADD_BASE[stage] + START))
                            stand_alone(pe, tensor_passed)
                        last = unit_half(k, half, unit_slot(unit, stage), bank_sum[s], starts, ends)
                        if half == 1:
                            last.then_inc(unit_used, 1)

            pe.sem_inc(unit_used, START)
            stages(pe, row_block)
            pe.wait_ge(neigh_copied, RB)
            pe.wait_ge(z_biased, RB - 1 + START)
            z_product(neigh, bank_z)

            def whole_unit(u, k, slot, bank, starts, ends, emptied, count):
                pe.wait_ge(x1_ready, (k + 1) * RPS + START)
                pe.wait_ge(unit_unpacked, u + (UNIT_BASE[NS] + 1))
                if starts:
                    pe.wait_ge(emptied, count)
                stand_alone(pe, tensor_passed)
                for half in range(2):
                    last = unit_half(k, half, slot, bank, starts and half == 0, ends and half == 1)
                last.then_inc(unit_used, 1)

            def tail_z(e, t, copied, count):
                pe.wait_ge(copied, count)
                pe.wait_ge(z_biased, t + (RB - 1 + START))
                z_product(neigh_t[e], bank_first if e else bank_z)

            pe.wait_ge(acc_added, ADD_BASE[NS] + START)
            for t in range(RPS):
                for k in range(NS):
                    u = NS * t + k
                    whole_unit(u, k, unit_slot(u, NS), bank_sum[t % 2], k == 0, k == NS - 1,
                               acc_copied, COPY_BASE[NS] + max(t - 1, 0) + START)
                    if t and k == 0:
                        tail_z((t - 1) % 2, t - 1, acc_copied, COPY_BASE[NS] + t + START)
            pe.wait_ge(flag_steps, 4)
            nc.tensor.matmul(bank_flag[0:1, 0:1], found[:, 2:3], ones[:, :], start=True, stop=True)\
              .then_inc(flag_summed, 1)

            with pe.Fori(0, (RB - RPS) // 2) as i:
                for e in range(2):
                    j = i * 2 + e
                    whole_unit(j + NS * RPS, NS - 1, unit_slot(e, NS), bank_sum[e], True, True,
                               acc_added, j + (ADD_BASE[NS] - 1 + START))
                    pe.wait_ge(acc_copied, COPY_BASE[NS] + RPS + START)
                    tail_z(1 - e, j + (RPS - 1), acc_added, j + (ADD_BASE[NS] + START))
            tail_z(1, RB - 1, acc_added, ADD_BASE[NS] + (RB - RPS) + START)

            pe.wait_ge(flag_ready, 1)
            general = pe.value_load(flag[0:1, 0:1], min_val=0, max_val=1)
            with pe.If(general == 1):
                pe.sem_inc(g_chunk_used, SLOTS)
                for rnd in range(2):
                    source = g_x1 if rnd else g_h
                    with pe.Fori(0, RB) as rb:
                        done = rb + rnd * RB
                        pe.wait_ge(g_h_ready, LN_PIECES)
                        if rnd:
                            pe.wait_ge(g_swished, RB + START)
                        pe.wait_ge(g_copied, done + START)
                        for c in range(CH):
                            pe.wait_ge(g_chunk_loaded[c % SLOTS],
                                       rb * (16 * CH // SLOTS) + 16 * (rnd * RB * CH // SLOTS + c // SLOTS + 1))
                            for t in range(TPC):
                                last = nc.tensor.matmul(bank_first[:, :], source[:, c * TPC + t, :],
                                                        ring[:, c % SLOTS, t * NB:(t + 1) * NB],
                                                        start=c == 0 and t == 0,
                                                        stop=c == CH - 1 and t == TPC - 1)
                            last.then_inc(g_chunk_used, 1)
                        pe.wait_ge(g_copied, done + (1 + START))
                        pe.wait_ge(g_biased, done + START)
                        z_product(neigh, bank_z, g_z_summed)


def kernel(x, adj, L0_gnn_W, L0_gnn_b):
    import numpy as np
    import concourse.bacc as bacc
    from concourse.bass_utils import run_bass_kernel_spmd

    x, w, b = (np.ascontiguousarray(a) for a in (x, L0_gnn_W, L0_gnn_b))
    blocks = np.asarray(adj).reshape(P, RB, TPB, P, CH, TPC).transpose(1, 4, 3, 5, 2, 0)
    adj_blocks = np.ascontiguousarray(blocks).reshape(RB, CH, P, CHUNK)

    nc = bacc.Bacc("TRN2", target_bir_lowering=False, num_devices=1)
    arrays = {"x_dram": x, "adj_dram": adj_blocks, "w_dram": w, "b_dram": b}
    args = [nc.dram_tensor(name, a.shape, mybir.dt.from_np(a.dtype), kind="ExternalInput").ap()
            for name, a in arrays.items()]
    out = nc.dram_tensor("out_dram", x.shape, mybir.dt.float32, kind="ExternalOutput").ap()
    graph_block(nc, *args, out)
    r = run_bass_kernel_spmd(nc, [arrays], core_ids=[0])
    return r.results[0]["out_dram"]
```

```python
from contextlib import ExitStack

import concourse.bass as bass
from concourse import mybir

P = 128
N = 8192
U = 128
KT = N // P
NB = 512
RB = N // NB
TPB = NB // P
TPC = 4
CHUNK = TPC * NB
CH = KT // TPC
GT = 8
GR = KT // GT
SLOTS = 4
F8_SLOTS = 4
NS = GR
RPS = RB // NS
WORDS = NB // 4
ONE8 = 2.0
PART_SCALE = 256.0
UNSCALE = 1.0 / (ONE8 * PART_SCALE)
LIMIT = 32768.0 / PART_SCALE
EPS = 1e-5
START = 2
X_LOADS = 4
LOAD_T = KT // X_LOADS
LN_PIECES = GR
LN_T = KT // LN_PIECES

GROUP_ORDER = [[0, 1, 2, 3, 4, 5, 6, 7], [1, 2, 3, 4, 0, 5, 6, 7], [2, 3, 4, 0, 5, 6, 1, 7],
               [3, 4, 0, 5, 1, 6, 2, 7], [4, 0, 5, 1, 6, 2, 7, 3], [5, 0, 6, 1, 7, 2, 3, 4],
               [6, 0, 1, 7, 2, 3, 4, 5], [7, 0, 1, 2, 3, 4, 5, 6]]
UNITS = [[], [((0,), 0)], [((1,), 0), ((1,), 1)], [((2,), 0), ((2,), 1)],
         [((3,), 0), ((2, 3), 2)], [((3,), 1), ((3,), 3)],
         [((4, 5), 0), ((4, 5), 2)], [((4, 5), 1), ((4, 5), 3)]]
UNITS_AFTER = [[], [5], [3, 5], [4, 6], [3, 4, 6], [2, 4], [2, 3, 3, 4], [1, 2, 2, 3]]
ACC_STAGE = 1
DIRECT_LAST = 4
TAIL_ITEMS = [(rb, {4: [(4, 5), (6, 7)], 5: [(5,), (6, 7)], 7: [(7,)]}.get(n, [(6, 7)]))
              for n in (4, 5, 7, 6, 3, 2, 1, 0) for rb in range(RPS * n + RPS - 1, RPS * n - 1, -1)]
TAIL_UNITS = [(t, i) for t, (_, units) in enumerate(TAIL_ITEMS) for i in range(len(units))]
TAIL_UNITS[1], TAIL_UNITS[2] = TAIL_UNITS[2], TAIL_UNITS[1]
TAIL_ALIKE = 6

UNIT_BASE = [RPS * sum(len(UNITS[s]) for s in range(stage)) for stage in range(NS + 1)]
ADDS = [len(units) - (stage == ACC_STAGE) for stage, units in enumerate(UNITS)]
ADD_BASE = [RPS * sum(ADDS[:stage]) for stage in range(NS + 1)]


def is_direct(stage, position):
    return GROUP_ORDER[stage][position] < stage


def packed_groups(stage, positions=GR):
    return sum(not is_direct(stage, p) for p in range(positions))


PACK_BASE = [3 * RPS * sum(packed_groups(s) for s in range(stage)) for stage in range(NS + 1)]


def packed_slot(g, n):
    return sum(GR - i for i in range(n)) + g - n


def graph_block(nc, x, adj, w, b, out):
    f32, f16, f8 = mybir.dt.float32, mybir.dt.float16, mybir.dt.float8e4
    u32 = mybir.dt.uint32
    ALU = mybir.AluOpType
    ACT = mybir.ActivationFunctionType

    x_v = x.rearrange("(p t) u -> p t u", t=KT)
    out_v = out.rearrange("(p t) u -> p t u", t=KT)

    ctx = ExitStack()
    with ctx:
        def sb(name, shape, dt):
            return ctx.enter_context(nc.sbuf_tensor(name, shape, dt))

        def pb(name):
            return ctx.enter_context(nc.psum_tensor(name, [P, NB], f32))

        def sem(name):
            return ctx.enter_context(nc.semaphore(name))

        ring = sb("adj_ring", [P, SLOTS, CHUNK], f32)
        x_all = ring[:, :, :].rearrange("p s (t u) -> p (s t) u", u=U)
        f8ring = sb("f8_ring", [P, F8_SLOTS, GT * NB], f8)
        packed = sb("packed", [P, GR * (GR + 1) // 2, RPS, WORDS], u32)
        h_parts = sb("h_parts", [P, 2, KT, U], f16)
        h_hi, h_lo = h_parts[:, 0], h_parts[:, 1]
        x1_parts = sb("x1_parts", [P, 2, KT, U], f16)
        x1_hi, x1_lo = x1_parts[:, 0], x1_parts[:, 1]
        acc = sb("acc", [P, RB, NB], f32)
        x_stage = acc[:, :, :].rearrange("p b n -> p (b n)")\
            .rearrange("p (t u) -> p t u", u=U)
        unpacked = sb("unpacked", [P, 2, GT, 2, WORDS], u32)
        folded = sb("folded", [P, 4 * WORDS], u32)
        folded_twice = sb("folded_twice", [P, 2 * WORDS], u32)
        w_sb = sb("w_sb", [P, U], f32)
        b_sb = sb("b_sb", [P, U], f32)
        neigh = sb("neigh", [P, NB], f32)
        act = neigh
        ln_space = unpacked[:, 0].rearrange("p t h w -> p (t h w)").bitcast(f32)
        stats = ln_space[:, 0:6 * KT].rearrange("p (t s) -> p t s", s=6)
        ln_a, ln_b, ln_c, ln_r, ln_n = (ln_space[:, (6 + i) * KT:(7 + i) * KT] for i in range(5))
        strays = sb("strays", [P, RB * CH], f32)
        tops = sb("tops", [P, 1], f32)
        found = sb("found", [P, 4], f32)
        ones = sb("ones", [P, 1], f32)
        flag = sb("flag", [1, 1], u32)
        neigh_t = [f8ring[:, i].bitcast(f32)[:, 0:NB] for i in range(2)]
        act_t = [f8ring[:, 2 + i].bitcast(f32)[:, 0:NB] for i in range(2)]

        g_h = h_parts[:, :, :, :].rearrange("p a t u -> p (a t u)").bitcast(f32)\
            .rearrange("p (t u) -> p t u", u=U)
        g_x1 = x1_parts[:, :, :, :].rearrange("p a t u -> p (a t u)").bitcast(f32)\
            .rearrange("p (t u) -> p t u", u=U)
        g_act = act_t[0]

        bank_first = pb("bank_first")
        bank_z = pb("bank_z")
        bank_sum = [pb(f"bank_sum{i}") for i in range(3)]
        bank_flag = pb("bank_flag")

        x_loaded = [sem(f"x_loaded{i}") for i in range(X_LOADS)]
        w_loaded = sem("w_loaded")
        chunk_loaded = [sem(f"chunk_loaded{i}") for i in range(SLOTS)]
        f8_made = sem("f8_made")
        chunk_checked = sem("chunk_checked")
        pack_steps = sem("pack_steps")
        ln_steps = sem("ln_steps")
        ln_vars = sem("ln_vars")
        ln_roots = sem("ln_roots")
        ln_scales = sem("ln_scales")
        h_scaled = sem("h_scaled")
        h_fp32 = sem("h_fp32")
        h_high = sem("h_high")
        h_ready = sem("h_ready")
        groups_done = sem("groups_done")
        first_summed = sem("first_summed")
        neigh_copied = sem("neigh_copied")
        z_summed = sem("z_summed")
        z_biased = sem("z_biased")
        act_done = sem("act_done")
        x1_high = sem("x1_high")
        x1_widened = sem("x1_widened")
        x1_ready = sem("x1_ready")
        unit_unpacked = sem("unit_unpacked")
        unit_used = sem("unit_used")
        direct_copied = sem("direct_copied")
        acc_started = sem("acc_started")
        acc_added = sem("acc_added")
        residual_added = sem("residual_added")
        x_reloaded = sem("x_reloaded")
        out_stored = sem("out_stored")
        scalar_passed = sem("scalar_passed")
        tensor_passed = sem("tensor_passed")
        vector_passed = sem("vector_passed")
        sync_passed = sem("sync_passed")
        pool_passed = sem("pool_passed")
        flag_steps = sem("flag_steps")
        flag_summed = sem("flag_summed")
        flag_ready = sem("flag_ready")

        g_x_loaded = [sem(f"g_x_loaded{i}") for i in range(X_LOADS)]
        g_ln_steps = sem("g_ln_steps")
        g_ln_vars = sem("g_ln_vars")
        g_ln_roots = sem("g_ln_roots")
        g_ln_scales = sem("g_ln_scales")
        g_h_scaled = sem("g_h_scaled")
        g_h_ready = sem("g_h_ready")
        g_chunk_loaded = [sem(f"g_chunk_loaded{i}") for i in range(SLOTS)]
        g_chunk_used = sem("g_chunk_used")
        g_copied = sem("g_copied")
        g_biased = sem("g_biased")
        g_swished = sem("g_swished")
        g_z_summed = sem("g_z_summed")
        g_x_reloaded = sem("g_x_reloaded")
        g_added = sem("g_added")
        g_stored = sem("g_stored")

        def f8_tile(group_slot, t):
            return f8ring[:, group_slot, t * NB:(t + 1) * NB]

        def unit_tile(slot, i, t):
            return unpacked[:, slot, t, i, :].bitcast(f8)

        def tiles(buf, rb):
            return buf[:, bass.ds(rb * TPB, TPB), :]

        def as_tiles(buf):
            return buf.rearrange("p (t u) -> p t u", u=U)

        def stand_alone(eng, passed):
            eng.sem_inc(passed, 1)

        def unit_slot(u, stage):
            return 1 if stage < NS and len(UNITS[stage]) == 1 else u % 2

        def units_at(stage, position):
            parts = [(u, i) for u, (groups, _) in enumerate(UNITS[stage]) for i in range(len(groups))]
            return [part for part, p in zip(parts, UNITS_AFTER[stage]) if p == position]

        def at_start(r):
            return isinstance(r, int) and r == 0

        def stages(eng, body, alone=(0,)):
            for stage in range(NS):
                if stage in alone:
                    for r in range(RPS):
                        body(stage, r)
                else:
                    with eng.Fori(0, RPS) as r:
                        body(stage, r)

        block = ctx.enter_context(nc.Block())

        @block.sync
        def _(sp):
            for i in range(X_LOADS):
                sp.dma_start(x_stage[:, i * LOAD_T:(i + 1) * LOAD_T, :],
                             x_v[:, i * LOAD_T:(i + 1) * LOAD_T, :]).then_inc(x_loaded[i], 16)

            def loads(stage, r):
                first = stage == 0 and at_start(r)
                rb = r + RPS * stage
                for c in range(CH):
                    if first and c == SLOTS:
                        sp.dma_start(w_sb[:, :], w).then_inc(w_loaded, 16)
                        sp.dma_start(b_sb[:, :], b.partition_broadcast(P)).then_inc(w_loaded, 16)
                    if not (first and c < SLOTS):
                        sp.wait_ge(chunk_checked, rb * CH + (c - SLOTS + 1))
                        stand_alone(sp, sync_passed)
                    chunk = 2 * GROUP_ORDER[stage][c // 2] + c % 2
                    sp.dma_start(ring[:, c % SLOTS, :], adj[rb, chunk]).then_inc(chunk_loaded[c % SLOTS], 16)

            stages(sp, loads)
            sp.wait_ge(chunk_checked, RB * CH)
            sp.dma_start(x_all, x_v).then_inc(x_reloaded, 16)

            for t, (rb, _) in enumerate(TAIL_ITEMS):
                sp.wait_ge(residual_added, t + 1)
                sp.dma_start(tiles(out_v, rb), tiles(x_all, rb)).then_inc(out_stored, 16)
            sp.wait_ge(out_stored, 16 * RB)

            sp.wait_ge(flag_ready, 1)
            general = sp.value_load(flag[0:1, 0:1], min_val=0, max_val=1)
            with sp.If(general == 1):
                for i in range(X_LOADS):
                    s = slice(i * LOAD_T, (i + 1) * LOAD_T)
                    sp.dma_start(g_h[:, s, :], x_v[:, s, :]).then_inc(g_x_loaded[i], 16)
                for rnd in range(2):
                    with sp.Fori(0, RB) as rb:
                        for c in range(CH):
                            sp.wait_ge(g_chunk_used, rb * CH + (rnd * RB * CH + c + 1))
                            sp.dma_start(ring[:, c % SLOTS, :], adj[rb, c])\
                              .then_inc(g_chunk_loaded[c % SLOTS], 16)
                    if rnd == 0:
                        sp.wait_ge(g_chunk_used, RB * CH + SLOTS)
                        sp.dma_start(g_h, x_v).then_inc(g_x_reloaded, 16)

        @block.scalar
        def _(sc):
            def ln_root(variances, roots):
                sc.wait_ge(variances, 1)
                nc.scalar.activation(ln_c, ln_b, ACT.Sqrt).then_inc(roots, 1)

            def high_part(i):
                s = slice(i * LN_T, (i + 1) * LN_T)
                sc.wait_ge(h_scaled, i + 1)
                nc.scalar.activation(x_stage[:, s, :], x_stage[:, s, :], ACT.Relu).then_inc(h_fp32, 1)
                sc.wait_ge(h_fp32, i + 1)
                nc.scalar.activation(h_hi[:, s, :], x_stage[:, s, :], ACT.Copy).then_inc(h_high, 1)

            def copy_neigh(stage, r, done):
                if stage > DIRECT_LAST or (stage == DIRECT_LAST and not at_start(r)):
                    sc.wait_ge(first_summed, done - DIRECT_LAST * RPS)
                else:
                    sc.wait_ge(groups_done, done * GR)
                sc.wait_ge(x1_ready, done - 1 + START)
                nc.scalar.activation(neigh[:, :], bank_first[:, :], ACT.Copy, scale=UNSCALE)\
                  .then_inc(neigh_copied, 1)

            def swish(done):
                sc.wait_ge(z_biased, done + START)
                nc.scalar.activation(act[:, :], act[:, :], ACT.Silu).then_inc(act_done, 1)
                sc.wait_ge(act_done, done)
                nc.scalar.activation(tiles(x1_hi, done - 1), as_tiles(act[:, :]), ACT.Copy,
                                     scale=PART_SCALE).then_inc(x1_high, 1)

            def copy_direct(rb):
                sc.wait_ge(groups_done, rb * GR + GR)
                nc.scalar.activation(acc[:, bass.ds(rb, 1), :], bank_sum[0][:, :], ACT.Copy,
                                     scale=UNSCALE).then_inc(direct_copied, 1)

            def row_block(stage, r):
                first = stage == 0 and at_start(r)
                rb = r + RPS * stage
                for p in range(GR):
                    if first and p == 0:
                        ln_root(ln_vars, ln_roots)
                    for half in range(2):
                        c = 2 * p + half
                        if half == 0 and not (first and p < F8_SLOTS):
                            sc.wait_ge(groups_done, rb * GR + (p - F8_SLOTS + 1))
                        sc.wait_ge(chunk_loaded[c % SLOTS], rb * (16 * CH // SLOTS) + 16 * (c // SLOTS + 1))
                        stand_alone(sc, scalar_passed)
                        nc.scalar.activation(f8ring[:, p % F8_SLOTS, half * CHUNK:(half + 1) * CHUNK],
                                             ring[:, c % SLOTS, :], ACT.Copy, scale=ONE8,
                                             saturate=False).then_inc(f8_made, 1)
                    if first:
                        high_part(p)
                    if p == 0 and not first:
                        copy_neigh(stage, r, rb)
                        if stage > 1 or (stage == 1 and not at_start(r)):
                            copy_direct(rb - 1)
                    if p == 2 and not first:
                        swish(rb)
                if stage == ACC_STAGE:
                    sc.wait_ge(unit_used, r * len(UNITS[stage]) + (UNIT_BASE[stage] + 1 + START))
                    nc.scalar.activation(acc[:, bass.ds(r, 1), :], bank_sum[1][:, :],
                                         ACT.Copy, scale=UNSCALE).then_inc(acc_started, 1)

            for started in (direct_copied, acc_started):
                sc.sem_inc(started, START)
            stages(sc, row_block, alone=(0, 1, DIRECT_LAST))
            copy_neigh(NS, 0, RB)
            copy_direct(RB - 1)
            swish(RB)

            for t in range(RB):
                sc.wait_ge(z_biased, RB + t + 1 + START)
                nc.scalar.activation(act_t[t % 2], act_t[t % 2], ACT.Silu).then_inc(act_done, 1)

            sc.wait_ge(flag_ready, 1)
            general = sc.value_load(flag[0:1, 0:1], min_val=0, max_val=1)
            with sc.If(general == 1):
                sc.sem_inc(g_copied, START)
                sc.sem_inc(g_swished, START)
                ln_root(g_ln_vars, g_ln_roots)
                for i in range(LN_PIECES):
                    part = g_h[:, i * LN_T:(i + 1) * LN_T, :]
                    sc.wait_ge(g_h_scaled, i + 1)
                    nc.scalar.activation(part, part, ACT.Relu).then_inc(g_h_ready, 1)
                for rnd in range(2):
                    with sc.Fori(0, RB) as rb:
                        done = rb + rnd * RB
                        sc.wait_ge(g_chunk_used, rb * CH + ((rnd * RB + 1) * CH + SLOTS))
                        nc.scalar.activation(neigh[:, :], bank_first[:, :], ACT.Copy).then_inc(g_copied, 1)
                        sc.wait_ge(g_biased, done + (1 + START))
                        to = as_tiles(g_act) if rnd else tiles(g_x1, rb)
                        nc.scalar.activation(to, as_tiles(g_act), ACT.Silu).then_inc(g_swished, 1)
                        if rnd:
                            sc.wait_ge(g_added, rb + 1)
                            sc.dma_start(tiles(out_v, rb), tiles(g_h, rb)).then_inc(g_stored, 16)
                sc.wait_ge(g_stored, 16 * RB)

        @block.gpsimd
        def _(po):
            def scale_rows(part_of, i, scaled):
                for t in range(i * LN_T, (i + 1) * LN_T):
                    row = part_of[:, t, :]
                    last = nc.gpsimd.tensor_scalar(row, row, ln_r[:, t:t + 1], ln_n[:, t:t + 1],
                                                   ALU.mult, ALU.add)
                last.then_inc(scaled, 1)

            def low_part(i):
                po.wait_ge(h_high, i + 1)
                s = slice(i * LN_T, (i + 1) * LN_T)
                nc.gpsimd.tensor_tensor(h_lo[:, s, :], x_stage[:, s, :], h_hi[:, s, :], ALU.subtract)\
                  .then_inc(h_ready, 1)

            def low_x1(done):
                po.wait_ge(x1_high, done)
                stand_alone(po, pool_passed)
                nc.gpsimd.tensor_scalar(act[:, :], act[:, :], PART_SCALE, None, ALU.mult)\
                  .then_inc(x1_widened, 1)
                po.wait_ge(x1_widened, done)
                nc.gpsimd.tensor_tensor(tiles(x1_lo, done - 1), as_tiles(act[:, :]),
                                        tiles(x1_hi, done - 1), ALU.subtract).then_inc(x1_ready, 1)

            po.sem_inc(x1_ready, START)
            po.wait_ge(ln_scales, 1)
            scale_rows(x_stage, 0, h_scaled)
            for i in range(LN_PIECES):
                if i + 1 < LN_PIECES:
                    scale_rows(x_stage, i + 1, h_scaled)
                low_part(i)
            with po.Fori(1, RB + 1) as done:
                low_x1(done)

            po.wait_ge(flag_ready, 1)
            general = po.value_load(flag[0:1, 0:1], min_val=0, max_val=1)
            with po.If(general == 1):
                po.wait_ge(g_ln_scales, 1)
                for i in range(LN_PIECES):
                    scale_rows(g_h, i, g_h_scaled)

        @block.vector
        def _(ve):
            def statistics(source, factor, loaded, counted, variances, roots, scales):
                steps = [0]

                def link(instruction):
                    instruction.then_inc(counted, 1)
                    steps[0] += 1
                    ve.wait_ge(counted, steps[0])

                for t in range(KT):
                    if t % LOAD_T == 0:
                        ve.wait_ge(loaded[t // LOAD_T], 16)
                    last = nc.vector.bn_stats(stats[:, t, :], source[:, t, :])
                link(last)
                nc.vector.tensor_tensor(ln_a, stats[:, :, 1], stats[:, :, 4], ALU.subtract)
                nc.vector.tensor_tensor(ln_n, stats[:, :, 1], stats[:, :, 4], ALU.add)
                link(nc.vector.tensor_tensor(ln_b, stats[:, :, 2], stats[:, :, 5], ALU.add))
                link(nc.vector.scalar_tensor_tensor(out=ln_a, in0=ln_a, scalar=0.25, in1=ln_a,
                                                    op0=ALU.mult, op1=ALU.mult))
                link(nc.vector.scalar_tensor_tensor(out=ln_b, in0=ln_b, scalar=1.0 / U, in1=ln_a,
                                                    op0=ALU.mult, op1=ALU.add))
                nc.vector.tensor_scalar(ln_b, ln_b, EPS, None, ALU.add).then_inc(variances, 1)
                ve.wait_ge(roots, 1)
                link(nc.vector.reciprocal(ln_r, ln_c))
                link(nc.vector.tensor_scalar(ln_r, ln_r, factor, None, ALU.mult))
                nc.vector.scalar_tensor_tensor(out=ln_n, in0=ln_n, scalar=-0.5, in1=ln_r,
                                               op0=ALU.mult, op1=ALU.mult).then_inc(scales, 1)

            def check(rb, c):
                ve.wait_ge(f8_made, rb * CH + (c + 1))
                word = ring[:, c % SLOTS, :]
                nc.vector.scalar_tensor_tensor(out=word, in0=word, scalar=1.0, in1=word,
                                               op0=ALU.is_equal, op1=ALU.not_equal,
                                               accum_out=strays[:, bass.ds(rb * CH + c, 1)])\
                  .then_inc(chunk_checked, 1)

            def fold(to, high, low, shift, by):
                nc.vector.scalar_tensor_tensor(out=to, in0=high, scalar=by, in1=low, op0=shift,
                                               op1=ALU.bitwise_or).then_inc(pack_steps, 1)

            def packs_before(stage, r, p):
                return r * (3 * packed_groups(stage)) + (PACK_BASE[stage] + 3 * packed_groups(stage, p))

            def pack_1(stage, r, p):
                done = packs_before(stage, r, p)
                if not (isinstance(done, int) and done == 0):
                    ve.wait_ge(pack_steps, done - 1)
                src = f8ring[:, p % F8_SLOTS, :].bitcast(u32)
                fold(folded[:, :], src[:, 4 * WORDS:], src[:, :4 * WORDS], ALU.logical_shift_right, 4)

            def pack_2(stage, r, p):
                ve.wait_ge(pack_steps, packs_before(stage, r, p) + 1)
                fold(folded_twice[:, :], folded[:, 2 * WORDS:], folded[:, :2 * WORDS],
                     ALU.logical_shift_right, 2)

            def pack_3(stage, r, p):
                ve.wait_ge(pack_steps, packs_before(stage, r, p) + 2)
                g = GROUP_ORDER[stage][p]
                fold(packed[:, packed_slot(g, stage), bass.ds(r, 1), :],
                     folded_twice[:, WORDS:], folded_twice[:, :WORDS], ALU.logical_shift_left, 1)

            def unpack(slot, free, groups, n, r):
                ve.wait_ge(unit_used, free + START)
                first = packed_slot(groups[0], n)
                src = packed[:, first:first + len(groups), bass.ds(r, 1), :]
                for t in range(GT):
                    up = 4 * (t // 4) + 2 * (t // 2 % 2) - t % 2
                    shift = ALU.logical_shift_left if up >= 0 else ALU.logical_shift_right
                    last = nc.vector.tensor_scalar(unpacked[:, slot, t, 0:len(groups), :], src, abs(up),
                                                   0x40404040, shift, ALU.bitwise_and)
                last.then_inc(unit_unpacked, 1)

            def bias_x1(done):
                ve.wait_ge(z_summed, done)
                ve.wait_ge(z_biased, done - 1 + START)
                stand_alone(ve, vector_passed)
                nc.vector.tensor_tensor_reduce(out=as_tiles(act[:, :]), in0=as_tiles(bank_z[:, :]),
                                               in1=b_sb[:, None, :].broadcast_to([P, TPB, U]), scale=1.0,
                                               scalar=tops[:, :], op0=ALU.add, op1=ALU.max,
                                               accum_out=tops[:, :]).then_inc(z_biased, 1)

            def bias(done, to, bank):
                ve.wait_ge(z_summed, done)
                nc.vector.tensor_tensor(as_tiles(to), as_tiles(bank),
                                        b_sb[:, None, :].broadcast_to([P, TPB, U]), ALU.add)\
                  .then_inc(z_biased, 1)

            def add_sum(stage, r, u):
                m = UNITS[stage][u][1]
                ve.wait_ge(unit_used, r * len(UNITS[stage]) + (UNIT_BASE[stage] + u + 1 + START))
                if m:
                    ve.wait_ge(direct_copied, r + (RPS * (m - 1) + 1 + START))
                else:
                    ve.wait_ge(acc_started, RPS + START)
                ve.wait_ge(acc_added, ADD_BASE[stage] + START)
                to = acc[:, bass.ds(r + RPS * m, 1), :].rearrange("p a n -> p (a n)")
                nc.vector.scalar_tensor_tensor(out=to, in0=bank_sum[1 + u][:, :], scalar=UNSCALE,
                                               in1=to, op0=ALU.mult, op1=ALU.add)\
                  .then_inc(acc_added, 1)

            def row_block(stage, r):
                first = stage == 0 and at_start(r)
                rb = r + RPS * stage
                units = UNITS[stage]

                def unpacks(behind):
                    for u, i in units_at(stage, behind + 1):
                        if i == 0:
                            index = r * len(units) + (UNIT_BASE[stage] + u)
                            unpack(unit_slot(u, stage), index if len(units) == 1 else index - 1,
                                   *units[u], r)

                if stage:
                    ve.wait_ge(pack_steps, PACK_BASE[stage])
                if first:
                    statistics(x_stage, PART_SCALE, x_loaded, ln_steps, ln_vars, ln_roots, ln_scales)
                for p in range(GR):
                    check(rb, 2 * p)
                    if p and not is_direct(stage, p - 1):
                        pack_2(stage, r, p - 1)
                    check(rb, 2 * p + 1)
                    if p and not is_direct(stage, p - 1):
                        pack_3(stage, r, p - 1)
                    if not is_direct(stage, p):
                        pack_1(stage, r, p)
                    if p == 1 and not first:
                        bias_x1(rb)
                    unpacks(p)
                if not is_direct(stage, GR - 1):
                    pack_2(stage, r, GR - 1)
                    pack_3(stage, r, GR - 1)
                for u in range(len(units) - ADDS[stage], len(units)):
                    add_sum(stage, r, u)

            for started in (z_biased, acc_added):
                ve.sem_inc(started, START)
            nc.vector.memset(ones[:, :], 1.0)
            nc.vector.memset(tops[:, :], 0.0).then_inc(flag_steps, 1)
            ve.wait_ge(flag_steps, 1)
            stages(ve, row_block)
            ve.wait_ge(pack_steps, PACK_BASE[NS])
            ve.wait_ge(acc_added, ADD_BASE[NS] + START)

            def tail_unpack(u):
                t, i = TAIL_UNITS[u]
                rb, groups = TAIL_ITEMS[t][0], TAIL_ITEMS[t][1][i]
                unpack(unit_slot(u, NS), UNIT_BASE[NS] + u - 1, groups, rb // RPS, rb % RPS)

            def tail_sum(t):
                last_unit = TAIL_UNITS.index((t, len(TAIL_ITEMS[t][1]) - 1))
                ve.wait_ge(unit_used, UNIT_BASE[NS] + last_unit + 1 + START)
                ve.wait_ge(direct_copied, RB - RPS + START)
                ve.wait_ge(z_summed, RB + t - 1)
                nc.vector.scalar_tensor_tensor(out=neigh_t[t % 2], in0=bank_sum[1 + t % 2][:, :],
                                               scalar=UNSCALE, in1=acc[:, TAIL_ITEMS[t][0], :],
                                               op0=ALU.mult, op1=ALU.add).then_inc(acc_added, 1)

            def tail_bias(t):
                bias(RB + t + 1, act_t[t % 2], (bank_first if t % 2 else bank_z)[:, :])

            def residual(t):
                ve.wait_ge(act_done, RB + t + 1)
                ve.wait_ge(x_reloaded, 16)
                to = tiles(x_all, TAIL_ITEMS[t][0])
                nc.vector.tensor_tensor(to, as_tiles(act_t[t % 2]), to, ALU.add)\
                  .then_inc(residual_added, 1)

            tail_unpack(0)
            tail_unpack(1)
            bias_x1(RB)
            def step(n, instruction):
                instruction.then_inc(flag_steps, 1)
                ve.wait_ge(flag_steps, n + 1)

            ve.wait_ge(z_biased, RB + START)
            ve.wait_ge(chunk_checked, RB * CH)
            step(1, nc.vector.tensor_scalar(found[:, 0:1], tops[:, :], LIMIT, None, ALU.is_gt))
            step(2, nc.vector.tensor_scalar(strays[:, :], strays[:, :], 1.0, None, ALU.mult, ALU.add,
                                            accum_out=found[:, 1:2]))
            step(3, nc.vector.tensor_tensor(found[:, 2:3], found[:, 0:1], found[:, 1:2], ALU.add))

            for u, (t, i) in enumerate(TAIL_UNITS):
                if u + 2 < len(TAIL_UNITS):
                    tail_unpack(u + 2)
                if i < len(TAIL_ITEMS[t][1]) - 1:
                    if t > 1:
                        tail_bias(t - 1)
                        residual(t - 1)
                    continue
                tail_sum(t)
                if t and len(TAIL_ITEMS[t][1]) == 1 or t == 1:
                    tail_bias(t - 1)
                    residual(t - 1)
                if t == TAIL_ALIKE - 1:
                    ve.wait_ge(flag_summed, 1)
                    nc.vector.tensor_scalar(flag[:, :], bank_flag[0:1, 0:1], 0.0, None, ALU.not_equal)\
                      .then_inc(flag_ready, 1)
            tail_bias(RB - 1)
            residual(RB - 1)

            ve.wait_ge(flag_ready, 1)
            general = ve.value_load(flag[0:1, 0:1], min_val=0, max_val=1)
            with ve.If(general == 1):
                ve.sem_inc(g_biased, START)
                statistics(g_h, 1.0, g_x_loaded, g_ln_steps, g_ln_vars, g_ln_roots, g_ln_scales)
                for rnd in range(2):
                    with ve.Fori(0, RB) as rb:
                        done = rb + rnd * RB
                        ve.wait_ge(g_z_summed, done + 1)
                        ve.wait_ge(g_swished, done + START)
                        nc.vector.tensor_tensor(as_tiles(g_act), as_tiles(bank_z[:, :]),
                                                b_sb[:, None, :].broadcast_to([P, TPB, U]), ALU.add)\
                          .then_inc(g_biased, 1)
                        if rnd:
                            ve.wait_ge(g_swished, done + (1 + START))
                            ve.wait_ge(g_x_reloaded, 16)
                            nc.vector.tensor_tensor(tiles(g_h, rb), as_tiles(g_act), tiles(g_h, rb),
                                                    ALU.add).then_inc(g_added, 1)

        @block.tensor
        def _(pe):
            def z_product(source, bank, summed=z_summed):
                for t in range(TPB):
                    last = nc.tensor.matmul(bank[:, t * U:(t + 1) * U], source[:, t * P:(t + 1) * P],
                                            w_sb[:, :], start=True, stop=True)
                last.then_inc(summed, 1)

            def unit_group(g, i, slot, bank, starts, ends):
                for t in range(GT):
                    for part in (x1_hi, x1_lo):
                        last = nc.tensor.matmul(bank[:, :], part[:, g * GT + t, :], unit_tile(slot, i, t),
                                                start=starts and t == 0 and part is x1_hi,
                                                stop=ends and t == GT - 1 and part is x1_lo)
                return last

            def first_round(p, g, t):
                for part in (h_hi, h_lo):
                    last = nc.tensor.matmul(bank_first[:, :], part[:, g * GT + t, :],
                                            f8_tile(p % F8_SLOTS, t),
                                            start=p == 0 and t == 0 and part is h_hi,
                                            stop=p == GR - 1 and t == GT - 1 and part is h_lo)
                return last

            def second_round(stage, p, g, t):
                for part in (x1_hi, x1_lo):
                    last = nc.tensor.matmul(bank_sum[0][:, :], part[:, g * GT + t, :],
                                            f8_tile(p % F8_SLOTS, t),
                                            start=g == 0 and t == 0 and part is x1_hi,
                                            stop=g == stage - 1 and t == GT - 1 and part is x1_lo)
                return last

            def row_block(stage, r):
                first = stage == 0 and at_start(r)
                rb = r + RPS * stage
                for p in range(GR):
                    g = GROUP_ORDER[stage][p]
                    direct = is_direct(stage, p)
                    for t in range(GT):
                        if t % TPC == 0:
                            pe.wait_ge(h_ready, g + 1)
                            if p == 0 and t == 0 and not first:
                                pe.wait_ge(neigh_copied, rb)
                            if direct and g == 0 and t == 0:
                                pe.wait_ge(direct_copied, r + (RPS * (stage - 1) + START))
                            if direct and t == 0:
                                pe.wait_ge(x1_ready, (g + 1) * RPS + START)
                            pe.wait_ge(f8_made, rb * CH + (2 * p + t // TPC + 1))
                            stand_alone(pe, tensor_passed)
                        last = first_round(p, g, t)
                        if direct and p < GR - 1:
                            last = second_round(stage, p, g, t)
                    if p == GR - 1:
                        if direct:
                            last.then_inc(first_summed, 1)
                            for t in range(GT):
                                last = second_round(stage, p, g, t)
                    last.then_inc(groups_done, 1)
                    if p == 0 and not first:
                        if stage == 0:
                            pe.wait_ge(w_loaded, 32)
                        pe.wait_ge(z_biased, rb - 1 + START)
                        z_product(neigh, bank_z)
                    for u, i in units_at(stage, p):
                        groups = UNITS[stage][u][0]
                        pe.wait_ge(x1_ready, (groups[i] + 1) * RPS + START)
                        if i == 0:
                            index = r * len(UNITS[stage]) + (UNIT_BASE[stage] + u)
                            pe.wait_ge(unit_unpacked, index + 1)
                            if stage == ACC_STAGE and u == 0:
                                pe.wait_ge(acc_started, r + START)
                            else:
                                pe.wait_ge(acc_added, r * ADDS[stage] + (ADD_BASE[stage] + START))
                            if stage > ACC_STAGE:
                                pe.wait_ge(acc_started, RPS + START)
                        stand_alone(pe, tensor_passed)
                        last = unit_group(groups[i], i, unit_slot(u, stage), bank_sum[1 + u],
                                          i == 0, i == len(groups) - 1)
                        if i == len(groups) - 1:
                            last.then_inc(unit_used, 1)

            pe.sem_inc(unit_used, START)
            stages(pe, row_block)

            def tail_unit(u, groups, slot, e, starts, ends, t):
                pe.wait_ge(x1_ready, (groups[-1] + 1) * RPS + START)
                pe.wait_ge(unit_unpacked, u + (UNIT_BASE[NS] + 1))
                if starts:
                    before = max(t - 1, 0) if isinstance(t, int) else t - 1
                    pe.wait_ge(acc_added, before + (ADD_BASE[NS] + START))
                stand_alone(pe, tensor_passed)
                for i, g in enumerate(groups):
                    last = unit_group(g, i, slot, bank_sum[1 + e], starts and i == 0,
                                      ends and i == len(groups) - 1)
                last.then_inc(unit_used, 1)

            def tail_z(e, t):
                pe.wait_ge(acc_added, t + (ADD_BASE[NS] + 1 + START))
                pe.wait_ge(z_biased, t + (RB - 1 + START))
                z_product(neigh_t[e], bank_first if e else bank_z)

            first_alike = TAIL_UNITS.index((TAIL_ALIKE, 0))
            for u, (t, i) in enumerate(TAIL_UNITS[:first_alike]):
                units = TAIL_ITEMS[t][1]
                last = i == len(units) - 1
                tail_unit(u, units[i], u % 2, t % 2, i == 0, last, t)
                if u == 0:
                    pe.wait_ge(neigh_copied, RB)
                    pe.wait_ge(z_biased, RB - 1 + START)
                    z_product(neigh, bank_z)
                if t and (i == 0 if t > 1 else last):
                    tail_z((t - 1) % 2, t - 1)
            pe.wait_ge(flag_steps, 4)
            nc.tensor.matmul(bank_flag[0:1, 0:1], found[:, 2:3], ones[:, :], start=True, stop=True)\
              .then_inc(flag_summed, 1)

            with pe.Fori(0, (RB - TAIL_ALIKE) // 2) as i:
                for e in range(2):
                    t = i * 2 + (TAIL_ALIKE + e)
                    tail_unit(i * 2 + (first_alike + e), TAIL_ITEMS[-1][1][0], e, e, True, True, t)
                    tail_z(1 - e, t - 1)
            tail_z(1, RB - 1)

            pe.wait_ge(flag_ready, 1)
            general = pe.value_load(flag[0:1, 0:1], min_val=0, max_val=1)
            with pe.If(general == 1):
                pe.sem_inc(g_chunk_used, SLOTS)
                for rnd in range(2):
                    source = g_x1 if rnd else g_h
                    with pe.Fori(0, RB) as rb:
                        done = rb + rnd * RB
                        pe.wait_ge(g_h_ready, LN_PIECES)
                        if rnd:
                            pe.wait_ge(g_swished, RB + START)
                        pe.wait_ge(g_copied, done + START)
                        for c in range(CH):
                            pe.wait_ge(g_chunk_loaded[c % SLOTS],
                                       rb * (16 * CH // SLOTS) + 16 * (rnd * RB * CH // SLOTS + c // SLOTS + 1))
                            for t in range(TPC):
                                last = nc.tensor.matmul(bank_first[:, :], source[:, c * TPC + t, :],
                                                        ring[:, c % SLOTS, t * NB:(t + 1) * NB],
                                                        start=c == 0 and t == 0,
                                                        stop=c == CH - 1 and t == TPC - 1)
                            last.then_inc(g_chunk_used, 1)
                        pe.wait_ge(g_copied, done + (1 + START))
                        pe.wait_ge(g_biased, done + START)
                        z_product(neigh, bank_z, g_z_summed)


def kernel(x, adj, L0_gnn_W, L0_gnn_b):
    import numpy as np
    import concourse.bacc as bacc
    from concourse.bass_utils import run_bass_kernel_spmd

    x, w, b = (np.ascontiguousarray(a) for a in (x, L0_gnn_W, L0_gnn_b))
    blocks = np.asarray(adj).reshape(P, RB, TPB, P, CH, TPC).transpose(1, 4, 3, 5, 2, 0)
    adj_blocks = np.ascontiguousarray(blocks).reshape(RB, CH, P, CHUNK)

    nc = bacc.Bacc("TRN2", target_bir_lowering=False, num_devices=1)
    arrays = {"x_dram": x, "adj_dram": adj_blocks, "w_dram": w, "b_dram": b}
    args = [nc.dram_tensor(name, a.shape, mybir.dt.from_np(a.dtype), kind="ExternalInput").ap()
            for name, a in arrays.items()]
    out = nc.dram_tensor("out_dram", x.shape, mybir.dt.float32, kind="ExternalOutput").ap()
    graph_block(nc, *args, out)
    r = run_bass_kernel_spmd(nc, [arrays], core_ids=[0])
    return r.results[0]["out_dram"]
```
